# Optimizing a Trainium2 kernel written in Bass

```python
import numpy as np
import jax
import jax.numpy as jnp

def _softmax(x, axis=-1):
    return jax.nn.softmax(x, axis=axis)

def _gelu(x):
    return jax.nn.gelu(x, approximate=True)

def _silu(x):
    return jax.nn.silu(x)

def _sigmoid(x):
    return jax.nn.sigmoid(x)

def _layernorm(x, axis=-1, eps=1e-05):
    m = jnp.mean(x, axis=axis, keepdims=True)
    v = jnp.var(x, axis=axis, keepdims=True)
    return (x - m) / jnp.sqrt(v + eps)

def _scatter_add(tgt, idx, src, axis=0):
    return tgt.at[idx].add(src)

def _segment_sum(src, seg, n):
    return jax.ops.segment_sum(src, seg, n)
kernel_name = 'mk_perceiver_d1_seqx_r8_ebcdfc'

def setup_inputs(seed: int=0):
    np.random.seed(seed)
    _w = jnp.asarray

    def _rec_inputs():
        import jax
        import jax.numpy as jnp
        _rk = jax.random.key(seed)
        x = -0.000125 + 0.9999 * jax.random.normal(jax.random.fold_in(_rk, 1), (64, 64, 128), jnp.float32)
        _lenS = 64 - jax.random.randint(jax.random.fold_in(_rk, 7), (64,), 0, max(1, 64 // 4) + 1, jnp.int32)
        _lenS2 = 128 - jax.random.randint(jax.random.fold_in(_rk, 8), (64,), 0, max(1, 128 // 4) + 1, jnp.int32)
        _ctx_768P = jax.random.normal(jax.random.fold_in(_rk, 11), (64, 16, 96), jnp.float32)
        _ctx_768c = jax.random.dirichlet(jax.random.fold_in(_rk, 511), 0.3 * jnp.ones((16,), jnp.float32), (64, 128))
        _ctx_768t = jnp.einsum('bsk,bkd->bsd', _ctx_768c, _ctx_768P)
        _ctx_768t = _ctx_768t * jax.lax.rsqrt(jnp.mean(jnp.square(_ctx_768t)) + 1e-12) * 0.953939
        ctx_768 = 0.00272024 + 0.999456 * (_ctx_768t + 0.3 * jax.random.normal(jax.random.fold_in(_rk, 611), (64, 128, 96), jnp.float32))
        return (x, ctx_768)
    x, ctx_768 = _rec_inputs()

    def _L0_xattn_setup():
        import jax, jax.numpy as jnp
        import numpy as np
        B, N, M = (8, 512, 77)
        Q_DIM, CTX_DIM = (128, 96)
        H, D = (16, 64)
        INNER = H * D
        key = jax.random.key(seed)
        ks = jax.random.split(key, 7)
        x = jax.random.normal(ks[0], (B, N, Q_DIM), dtype=jnp.float32)
        context = jax.random.normal(ks[1], (B, M, CTX_DIM), dtype=jnp.float32)
        Wq = jax.random.normal(ks[2], (Q_DIM, INNER), dtype=jnp.float32) * Q_DIM ** (-0.5)
        Wk = jax.random.normal(ks[3], (CTX_DIM, INNER), dtype=jnp.float32) * CTX_DIM ** (-0.5)
        Wv = jax.random.normal(ks[4], (CTX_DIM, INNER), dtype=jnp.float32) * CTX_DIM ** (-0.5)
        Wo = jax.random.normal(ks[5], (INNER, Q_DIM), dtype=jnp.float32) * INNER ** (-0.5)
        bo = jax.random.normal(ks[6], (Q_DIM,), dtype=jnp.float32) * 0.01
        return {'x': x, 'context': context, 'Wq': Wq, 'Wk': Wk, 'Wv': Wv, 'Wo': Wo, 'bo': bo}
    _L0_xattn_all = _L0_xattn_setup()
    _L0_xattn_in = {k: v for k, v in _L0_xattn_all.items() if k in ('Wq', 'Wk', 'Wv', 'Wo', 'bo')}
    del _L0_xattn_all

    def _L0_attn_setup():
        import jax, jax.numpy as jnp
        import numpy as np
        D_MODEL = 128
        N_HEADS = 16
        TREE_DEPTH = 5
        B, T = (2, 128)
        key = jax.random.key(seed)
        k1, k2, k3, k4 = jax.random.split(key, 4)
        sc = 1.0 / np.sqrt(D_MODEL)
        return {'x': jax.random.normal(k1, (B, T, D_MODEL), dtype=jnp.float32), 'Wp': jax.random.normal(k2, (D_MODEL, N_HEADS * TREE_DEPTH), dtype=jnp.float32) * sc, 'bp': jnp.zeros((N_HEADS * TREE_DEPTH,), dtype=jnp.float32), 'Wv': jax.random.normal(k3, (D_MODEL, D_MODEL), dtype=jnp.float32) * sc, 'Wo': jax.random.normal(k4, (D_MODEL, D_MODEL), dtype=jnp.float32) * sc}
    _L0_attn_all = _L0_attn_setup()
    _L0_attn_in = {k: v for k, v in _L0_attn_all.items() if k in ('Wp', 'bp', 'Wv', 'Wo')}
    del _L0_attn_all

    def _L0_ffn_setup():
        import jax, jax.numpy as jnp
        import numpy as np
        D_IN = 128
        D_OUT = 128
        D_QUERY = 32
        N_HEADS = 8
        N_EXPERTS = 8192
        N_SQRT = 32
        TOPK = 10
        DQ_HALF = D_QUERY // 2
        key = jax.random.key(seed)
        ks = jax.random.split(key, 7)
        B, S = (2, 128)
        x = jax.random.normal(ks[0], (B, S, D_IN), dtype=jnp.float32)
        Wq = jax.random.normal(ks[1], (D_IN, D_QUERY * N_HEADS), dtype=jnp.float32) / np.sqrt(D_IN)
        bq = jnp.zeros((D_QUERY * N_HEADS,), dtype=jnp.float32)
        K1 = jax.random.normal(ks[2], (N_SQRT, DQ_HALF), dtype=jnp.float32)
        K2 = jax.random.normal(ks[3], (N_SQRT, DQ_HALF), dtype=jnp.float32)
        W_up = jax.random.normal(ks[4], (N_EXPERTS, D_OUT), dtype=jnp.float32)
        W_down = jax.random.normal(ks[5], (N_EXPERTS, D_IN), dtype=jnp.float32)
        return {'x': x, 'Wq': Wq, 'bq': bq, 'K1': K1, 'K2': K2, 'W_up': W_up, 'W_down': W_down}
    _L0_ffn_all = _L0_ffn_setup()
    _L0_ffn_in = {k: v for k, v in _L0_ffn_all.items() if k in ('Wq', 'bq', 'K1', 'K2', 'W_up', 'W_down')}
    del _L0_ffn_all
    return {'x': x, 'ctx_768': ctx_768, 'L0_xattn_Wq': _L0_xattn_in['Wq'], 'L0_xattn_Wk': _L0_xattn_in['Wk'], 'L0_xattn_Wv': _L0_xattn_in['Wv'], 'L0_xattn_Wo': _L0_xattn_in['Wo'], 'L0_xattn_bo': _L0_xattn_in['bo'], 'L0_attn_Wp': _L0_attn_in['Wp'], 'L0_attn_bp': _L0_attn_in['bp'], 'L0_attn_Wv': _L0_attn_in['Wv'], 'L0_attn_Wo': _L0_attn_in['Wo'], 'L0_ffn_Wq': _L0_ffn_in['Wq'], 'L0_ffn_bq': _L0_ffn_in['bq'], 'L0_ffn_K1': _L0_ffn_in['K1'], 'L0_ffn_K2': _L0_ffn_in['K2'], 'L0_ffn_W_up': _L0_ffn_in['W_up'], 'L0_ffn_W_down': _L0_ffn_in['W_down']}

def reference(x, ctx_768, L0_xattn_Wq, L0_xattn_Wk, L0_xattn_Wv, L0_xattn_Wo, L0_xattn_bo, L0_attn_Wp, L0_attn_bp, L0_attn_Wv, L0_attn_Wo, L0_ffn_Wq, L0_ffn_bq, L0_ffn_K1, L0_ffn_K2, L0_ffn_W_up, L0_ffn_W_down):
    import jax
    import jax.numpy as jnp

    def _L0_xattn_ref(x, context, Wq, Wk, Wv, Wo, bo):
        import jax, jax.numpy as jnp
        import numpy as np
        B, N, M = (8, 512, 77)
        Q_DIM, CTX_DIM = (128, 96)
        H, D = (16, 64)
        INNER = H * D
        scale = D ** (-0.5)

        def heads(t):
            b, s, _ = t.shape
            return t.reshape(b, s, H, D).transpose(0, 2, 1, 3)
        q = heads(x @ Wq)
        k = heads(context @ Wk)
        v = heads(context @ Wv)
        scores = jnp.einsum('bhid,bhjd->bhij', q, k) * scale
        attn = jax.nn.softmax(scores, axis=-1)
        out = jnp.einsum('bhij,bhjd->bhid', attn, v)
        out = out.transpose(0, 2, 1, 3).reshape(x.shape[0], x.shape[1], INNER)
        return out @ Wo + bo

    def _L0_attn_ref(x, Wp, bp, Wv, Wo):
        import jax, jax.numpy as jnp
        import numpy as np
        D_MODEL = 128
        N_HEADS = 16
        TREE_DEPTH = 5
        B, T = (2, 128)
        Bc, Tc, d = x.shape
        H, Dt = (N_HEADS, TREE_DEPTH)
        dh = d // H
        paths = jax.nn.sigmoid(x @ Wp + bp).reshape(Bc, Tc, H, Dt).transpose(0, 2, 1, 3)
        pq = paths[:, :, :, None, :]
        pk = paths[:, :, None, :, :]
        agree = pq * pk + (1.0 - pq) * (1.0 - pk)
        sim = jnp.cumprod(agree, axis=-1).sum(axis=-1) / Dt
        causal_mask = jnp.triu(jnp.ones((Tc, Tc), dtype=bool), k=1)
        sim = jnp.where(causal_mask[None, None], -jnp.inf, sim)
        attn = jax.nn.softmax(sim, axis=-1)
        V = (x @ Wv).reshape(Bc, Tc, H, dh).transpose(0, 2, 1, 3)
        ctx = jnp.einsum('bhqk,bhkd->bhqd', attn, V)
        ctx = ctx.transpose(0, 2, 1, 3).reshape(Bc, Tc, d)
        return ctx @ Wo

    def _L0_ffn_ref(x, Wq, bq, K1, K2, W_up, W_down):
        import jax, jax.numpy as jnp
        import numpy as np
        D_IN = 128
        D_OUT = 128
        D_QUERY = 32
        N_HEADS = 8
        N_EXPERTS = 8192
        N_SQRT = 32
        TOPK = 10
        DQ_HALF = D_QUERY // 2
        B, S, _ = x.shape
        q = (x @ Wq + bq).reshape(B, S, N_HEADS, D_QUERY)
        q1, q2 = (q[..., :DQ_HALF], q[..., DQ_HALF:])
        s1 = jnp.einsum('bshd,nd->bshn', q1, K1)
        s2 = jnp.einsum('bshd,nd->bshn', q2, K2)
        v1, i1 = jax.lax.top_k(s1, TOPK)
        v2, i2 = jax.lax.top_k(s2, TOPK)
        all_scores = (v1[..., :, None] + v2[..., None, :]).reshape(B, S, N_HEADS, TOPK * TOPK)
        all_indices = (i1[..., :, None] * N_SQRT + i2[..., None, :]).reshape(B, S, N_HEADS, TOPK * TOPK)
        vals, best = jax.lax.top_k(all_scores, TOPK)
        expert_idx = jnp.take_along_axis(all_indices, best, axis=-1)
        w_down = W_down[expert_idx]
        w_up = W_up[expert_idx]
        scores = jax.nn.softmax(vals, axis=-1)
        h = jnp.einsum('bsd,bshkd->bshk', x, w_down)
        h = jax.nn.gelu(h, approximate=False) * scores
        out = jnp.einsum('bshk,bshkd->bsd', h, w_up)
        return out
    x = x + _L0_xattn_ref(_layernorm(x, axis=-1), ctx_768, L0_xattn_Wq, L0_xattn_Wk, L0_xattn_Wv, L0_xattn_Wo, L0_xattn_bo)
    x = x + _L0_attn_ref(_layernorm(x, axis=-1), L0_attn_Wp, L0_attn_bp, L0_attn_Wv, L0_attn_Wo)
    x = x + _L0_ffn_ref(_layernorm(x, axis=-1), L0_ffn_Wq, L0_ffn_bq, L0_ffn_K1, L0_ffn_K2, L0_ffn_W_up, L0_ffn_W_down)
    return x

_drawn_inputs = setup_inputs


def setup_inputs(seed=0):
    import zlib

    import numpy as np

    out = dict(_drawn_inputs(seed))
    spreads = {'L0_attn_bp': (0.0, 2.0), 'L0_ffn_bq': (0.0, 0.1)}
    factors = {}
    for name, (base, spread) in spreads.items():
        noise = np.random.default_rng([zlib.crc32(name.encode()), seed]).standard_normal(out[name].shape)
        drawn = base * np.exp(spread * noise) if base else spread * noise
        out[name] = jnp.asarray(drawn.astype(out[name].dtype))
    for name, factor in factors.items():
        out[name] = (out[name] * factor).astype(out[name].dtype)
    return out
```

```python
from contextlib import ExitStack

import numpy as np
import concourse.bass as bass
from concourse import mybir

B, N, D = 64, 64, 128
M, CD = 128, 96
XH, XD = 16, 64
AH, DEPTH, AD = 16, 5, 8
NF = 2 ** DEPTH
FH, NSQ, TOPK, DQH = 8, 32, 10, 16
NE = NSQ * NSQ
PAIR = 2 * N
NT = B * N // PAIR
XHP = XH // 2
EC = NE // 128
NQ = 2 * FH
DROPPED = -3.0e38
FLOOR = -30000.0

CAND = [(TOPK + 1) // (i + 1) for i in range(TOPK + 1)]
NCAND = sum(CAND)


def build(nc, a):
    f32, f16 = mybir.dt.float32, mybir.dt.float16
    ALU, ACT, AX = mybir.AluOpType, mybir.ActivationFunctionType, mybir.AxisListType
    ctx = ExitStack()
    with ctx:
        def sb(name, shape, dt=f32):
            return ctx.enter_context(nc.sbuf_tensor(name, shape, dt))

        def sem(name):
            return ctx.enter_context(nc.semaphore(name))

        ident = sb("ident", [128, 128])
        ident16 = sb("ident16", [128, 128], f16)
        sel = sb("sel", [128, NE], f16)
        cmask = sb("cmask", [128, N])
        rootc = sb("rootc", [128, 1])
        ones = sb("ones", [1, 128])
        halfneg = sb("halfneg", [128, 1])
        wqT = sb("wqT", [128, XHP, D])
        wkT = sb("wkT", [128, XHP, CD])
        wvT = sb("wvT", [128, XHP, CD])
        wo = sb("wo", [128, XHP, D])
        bo = sb("bo", [1, D])
        wp = sb("wp", [D, AH * DEPTH])
        bp = sb("bp", [1, AH * DEPTH])
        awv = sb("awv", [D, D])
        awo = sb("awo", [D, D])
        fwqT = sb("fwqT", [128, 2, D])
        fbqT = sb("fbqT", [128, 2])
        keys = sb("keys", [128, 4, 2 * NSQ])
        wdT = sb("wdT", [D, NE])
        wup = sb("wup", [128, EC, D])
        qk = sb("qk", [D, XH, CD])
        vo = sb("vo", [CD, XH, D])
        fqk = sb("fqk", [D, FH * 2 * NSQ])
        fbk = sb("fbk", [1, FH * 2 * NSQ])
        x = sb("x", [128, D])
        c0 = sb("c0", [M, 2, CD])
        cT = sb("cT", [CD, 2, M])
        st = sb("st", [128, 6])
        mv = sb("mv", [128, 2])
        rstd = sb("rstd", [128, 1])
        xn = sb("xn", [128, D])
        xnT = sb("xnT", [D, 128])
        tT = sb("tT", [CD, 2, XH, N])
        negmax = sb("negmax", [128, 2, XHP])
        rowsum = sb("rowsum", [128, 2, XHP])
        rrow = sb("rrow", [128, 2, XHP])
        p = sb("p", [128, 2, XHP, M])
        pT = sb("pT", [M, 2, XH * N])
        uT = sb("uT", [CD, XH, 2, N])
        x2 = sb("x2", [128, D])
        st2 = sb("st2", [128, 6])
        mv2 = sb("mv2", [128, 2])
        rstd2 = sb("rstd2", [128, 1])
        xn2 = sb("xn2", [128, D])
        xn2T = sb("xn2T", [D, 128])
        alpha = sb("alpha", [128, AH, DEPTH])
        feat = sb("feat", [128, AH, NF])
        featT = sb("featT", [128, 4, 128])
        vblk = sb("vblk", [128, AH, 2, AD + 1])
        ap_ = sb("ap_", [128, 4, 4, N])
        am = sb("am", [128, 4, 4, N])
        arz = sb("arz", [N, AH, 2])
        actx = sb("actx", [N, 2, AH * AD])
        actxT = sb("actxT", [D, 128])
        x3 = sb("x3", [128, D])
        st3 = sb("st3", [128, 6])
        mv3 = sb("mv3", [128, 2])
        rstd3 = sb("rstd3", [128, 1])
        xn3 = sb("xn3", [128, D])
        xn3T = sb("xn3T", [D, 128])
        top = sb("top", [128, NQ, 16])
        tops = sb("tops", [128, NQ, 16])
        u = sb("u", [128, NQ, NSQ])
        u2 = sb("u2", [128, NQ, NSQ])
        us = sb("us", [128, FH, 2, 2 * NSQ], f16)
        usT = sb("usT", [128, FH, 128], f16)
        cand = sb("cand", [128, FH, NCAND])
        cand2 = sb("cand2", [128, FH, NCAND])
        best = sb("best", [128, FH, 16])
        cut = sb("cut", [128, FH])
        ebest = sb("ebest", [128, FH, TOPK])
        z = sb("z", [128, FH])
        rz = sb("rz", [128, FH])
        gh = sb("gh", [128, NE])
        ew = sb("ew", [128, 2, NE])
        mw = sb("mw", [128, 2, NE])
        wsum = sb("wsum", [128, NE])
        g = sb("g", [128, NE])
        gT = sb("gT", [128, EC, 128])
        y = sb("y", [128, D])

        psA = ctx.enter_context(nc.psum_tensor("psA", [128, 4, 512], f32))
        psF = ctx.enter_context(nc.psum_tensor("psF", [128, 4, 512], f32))
        a0 = psA[:, 0:2, :].rearrange("p a b -> p (a b)")
        a1 = psA[:, 2:4, :].rearrange("p a b -> p (a b)")
        f0 = psF[:, 0:2, :].rearrange("p a b -> p (a b)")
        f1 = psF[:, 2:4, :].rearrange("p a b -> p (a b)")
        aslot = [a0, a1]
        fslot = [f0, f1]

        names = """wload cload consts setup_ps setup_sb
            x_in c_in out_done
            dve_x dve_f pool_x var1 rstd1 xn_ready xnT_ps xnT_sb tT_ps tT0_sb tT1_sb
            sc_ps max_done exp_done rrow_done norm_done pT_ps pT_sb u_ps u0_sb u1_sb xo_ps x2_ready
            var2 rstd2_s xn2_ready xn2T_ps xn2T_sb pv_ps alpha_done v_sb feat_ready featT_ps featT_sb
            sim_ps sime am_done actx_ps actx_ready actxT_ps actxT_sb ao_ps var3 rstd3_s xn3_ready
            xn3T_ps xn3T_sb key_ps h_ps us_ready usT_ps usT_sb gelu_done best_ready ebest_done
            s_ps ew_done mw_done wsum_ready g_ready gT_ps gT_sb y_ps y_ready""".split()
        s = {n: sem(n) for n in names}
        loads = ctx.enter_context(nc.semaphore("loads"))
        block = ctx.enter_context(nc.Block())

        WEIGHTS = [(ident, a["ident"]), (ident16, a["ident16"]), (sel, a["sel"]), (cmask, a["cmask"]),
                   (rootc, a["rootc"]),
                   (wqT, a["wqT"].rearrange("(c p) d -> p c d", p=128)),
                   (wkT, a["wkT"].rearrange("(c p) d -> p c d", p=128)),
                   (wvT, a["wvT"].rearrange("(c p) d -> p c d", p=128)),
                   (wo, a["wo"].rearrange("(c p) d -> p c d", p=128)),
                   (bo, a["bo"]), (wp, a["wp"]), (bp, a["bp"]), (awv, a["awv"]), (awo, a["awo"]),
                   (fwqT, a["fwqT"].rearrange("(c p) d -> p c d", p=128)),
                   (fbqT, a["fbqT"]), (keys, a["keys"]), (wdT, a["wdT"]),
                   (wup, a["wup"].rearrange("(c p) d -> p c d", p=128))]
        xt = a["x"].rearrange("(t p) d -> t p d", p=128)
        ct = a["c"].rearrange("(t b) m c -> t m b c", b=2)
        ctT = a["cT"].rearrange("(t b) c m -> t c b m", b=2)
        yt = a["y"].rearrange("(t p) d -> t p d", p=128)

        def alternate(attention, experts, order):
            ia, ie = iter(attention), iter(experts)
            for k in order:
                yield next(ia) if k == "a" else next(ie)

        def run(eng, attention, experts, order, begin):
            assert order.count("a") == len(attention) and order.count("e") == len(experts)
            begin(0, None)
            for step in attention:
                step(0)

            def turn(t):
                begin(t, t - 1)
                for k, step in zip(order, alternate(attention, experts, order)):
                    step(t if k == "a" else t - 1)

            turn(1)
            with eng.Fori(2, NT) as t:
                turn(t)
            begin(None, NT - 1)
            for step in experts:
                step(NT - 1)

        def wait_past(eng, sm, count):
            if not (isinstance(count, int) and count <= 0):
                eng.wait_ge(sm, count)

        @block.sync
        def _(sp):
            for dst, src in WEIGHTS:
                sp.dma_start(dst[:], src).then_inc(s["wload"], 16)

            def load(t):
                sp.dma_start(x[:], xt[t]).then_inc(s["x_in"], 16)
                sp.dma_start(c0[:], ct[t]).then_inc(s["c_in"], 16)
                sp.dma_start(cT[:], ctT[t]).then_inc(s["c_in"], 16)

            load(0)
            with sp.Fori(1, NT) as t:
                sp.wait_ge(s["x2_ready"], t)
                sp.nop(nofuse=True)
                sp.wait_ge(s["u_ps"], 2 * t)
                sp.nop(nofuse=True)
                load(t)
                sp.wait_ge(s["y_ready"], t)
                sp.nop(nofuse=True)
                sp.dma_start(yt[t - 1], y[:]).then_inc(s["out_done"], 16)
            sp.wait_ge(s["y_ready"], NT)
            sp.dma_start(yt[NT - 1], y[:]).then_inc(s["out_done"], 16)
            sp.wait_ge(s["out_done"], 16 * NT)

        @block.tensor
        def _(pe):
            pe.wait_ge(s["wload"], 16 * len(WEIGHTS))
            pe.wait_ge(s["consts"], 1)

            def setup_round(n, mms):
                if n >= 1:
                    pe.wait_ge(s["setup_sb"], n)
                for out, lhsT, rhs in mms:
                    mm = pe.matmul(out, lhsT, rhs, start=True, stop=True)
                mm.then_inc(s["setup_ps"], 1)

            for j in range(4):
                mms = []
                for i in range(4):
                    h = 4 * j + i
                    r = 64 * (h % 2)
                    mms.append((psA[:, h % 2 + 2 * (j % 2), (i // 2) * CD:(i // 2 + 1) * CD],
                                wqT[r:r + 64, h // 2, :], wkT[r:r + 64, h // 2, :]))
                setup_round(j, mms)
            for j in range(4):
                mms = []
                for i in range(4):
                    h = 4 * j + i
                    r = 64 * (h % 2)
                    mms.append((psA[0:CD, h % 2 + 2 * (j % 2), (i // 2) * D:(i // 2 + 1) * D],
                                wvT[r:r + 64, h // 2, :], wo[r:r + 64, h // 2, :]))
                setup_round(4 + j, mms)
            kflat = keys[:].rearrange("p g i -> p (g i)")
            setup_round(8, [(f0[:, 256 * c:256 * c + 256], fwqT[:, c, :], kflat) for c in range(2)])
            setup_round(9, [(f1[0:1, 256 * c:256 * c + 256], fbqT[:, c:c + 1], kflat) for c in range(2)])
            pe.wait_ge(s["setup_sb"], 10)

            def xn_turn(t):
                pe.wait_ge(s["xn_ready"], t + 1)
                wait_past(pe, s["xn3_ready"], t)
                pe.transpose(a0[:, 0:128], xn[:], ident[:]).then_inc(s["xnT_ps"], 1)

            def queries(half):
                def step(t):
                    pe.wait_ge(s["xnT_sb"], t + 1)
                    wait_past(pe, s["actxT_sb"], t)
                    for i in range(8):
                        mm = pe.matmul(aslot[1 - half][0:CD, i * 128:i * 128 + 128], qk[:, 8 * half + i, :],
                                       xnT[:], start=True, stop=True)
                    mm.then_inc(s["tT_ps"], 1)
                return step

            def scores(b):
                def step(t):
                    pe.wait_ge(s["tT0_sb"], t + 1)
                    pe.wait_ge(s["tT1_sb"], t + 1)
                    pe.wait_ge(s["c_in"], 32 * (t + 1))
                    for k in range(XHP):
                        mm = pe.matmul(aslot[1 - b][:, k * M:k * M + M],
                                       tT[:, b, 2 * k:2 * k + 2, :].rearrange("c h q -> c (h q)"),
                                       cT[:, b, :], start=True, stop=True)
                    mm.then_inc(s["sc_ps"], 1)
                return step

            def probs_turn(b):
                def step(t):
                    pe.wait_ge(s["norm_done"], 2 * t + 1 + b)
                    for k in range(XHP):
                        mm = pe.transpose(aslot[1 - b][:, k * 128:k * 128 + 128], p[:, b, k, :], ident[:])
                    mm.then_inc(s["pT_ps"], 1)
                return step

            def mix(b):
                def step(t):
                    pe.wait_ge(s["pT_sb"], 2 * t + 1 + b)
                    for j in range(2):
                        mm = pe.matmul(aslot[1 - b][0:CD, j * 512:j * 512 + 512], c0[:, b, :],
                                       pT[:, b, j * 512:j * 512 + 512], start=True, stop=True)
                    mm.then_inc(s["u_ps"], 1)
                return step

            def cross_out(t):
                pe.wait_ge(s["u0_sb"], t + 1)
                pe.wait_ge(s["u1_sb"], t + 1)
                pe.matmul(a1[:, 0:D], ones[:], bo[:], start=True, stop=False)
                for h in range(XH):
                    mm = pe.matmul(a1[:, 0:D], uT[:, h, :, :].rearrange("c b q -> c (b q)"), vo[:, h, :],
                                   start=False, stop=(h == XH - 1))
                mm.then_inc(s["xo_ps"], 1)

            def xn2_turn(t):
                pe.wait_ge(s["xn2_ready"], t + 1)
                pe.transpose(a0[:, 0:128], xn2[:], ident[:]).then_inc(s["xn2T_ps"], 1)

            def paths_values(t):
                pe.wait_ge(s["xn2T_sb"], t + 1)
                pe.matmul(a1[:, 0:AH * DEPTH], ones[:], bp[:], start=True, stop=False)
                pe.matmul(a1[:, 0:AH * DEPTH], xn2T[:], wp[:], start=False, stop=True)
                pe.matmul(a1[:, 128:256], xn2T[:], awv[:], start=True, stop=True).then_inc(s["pv_ps"], 1)

            def feat_turn(t):
                pe.wait_ge(s["feat_ready"], t + 1)
                ff = feat[:].rearrange("p (c r) f -> p c (r f)", c=4)
                for c in range(4):
                    mm = pe.transpose(a0[:, c * 128:c * 128 + 128], ff[:, c, :], ident[:])
                mm.then_inc(s["featT_ps"], 1)

            def similarity(t):
                pe.wait_ge(s["featT_sb"], t + 1)
                pe.wait_ge(s["alpha_done"], t + 1)
                pe.wait_ge(s["v_sb"], 2 * (t + 1))
                for c in range(4):
                    for b in range(2):
                        for r in range(4):
                            ft = featT[32 * r:32 * r + 32, c, N * b:N * b + N]
                            mm = pe.matmul(psA[N * b:N * b + N, r, c * N:c * N + N], ft, ft,
                                           start=True, stop=True, tile_position=(32 * r, N * b))
                mm.then_inc(s["sim_ps"], 1)

            def tree_mix(t):
                pe.wait_ge(s["am_done"], t + 1)
                for h in range(AH):
                    mm = pe.matmul(a0[0:N, h * 18:h * 18 + 18], am[:, h % 4, h // 4, :],
                                   vblk[:, h, :, :].rearrange("p b d -> p (b d)"), start=True, stop=True)
                mm.then_inc(s["actx_ps"], 1)

            def tree_turn(t):
                pe.wait_ge(s["actx_ready"], t + 1)
                pe.nop(nofuse=True)
                for b in range(2):
                    mm = pe.transpose(a1[:, b * N:b * N + N], actx[:, b, :], ident[0:N, 0:N])
                mm.then_inc(s["actxT_ps"], 1)

            def tree_out(t):
                pe.wait_ge(s["actxT_sb"], t + 1)
                pe.matmul(a0[:, 0:D], actxT[:], awo[:], start=True, stop=True).then_inc(s["ao_ps"], 1)

            def xn3_turn(t):
                pe.wait_ge(s["xn3_ready"], t + 1)
                wait_past(pe, s["gT_sb"], t)
                pe.transpose(f0[:, 0:128], xn3[:], ident[:]).then_inc(s["xn3T_ps"], 1)

            def key_scores(t):
                pe.wait_ge(s["xn3T_sb"], t + 1)
                wait_past(pe, s["y_ready"], t)
                pe.matmul(f1[:, 0:512], ones[:], fbk[:], start=True, stop=False)
                pe.matmul(f1[:, 0:512], xn3T[:], fqk[:], start=False, stop=True).then_inc(s["key_ps"], 1)

            def hidden(t):
                for j in range(2):
                    mm = pe.matmul(f0[:, j * 512:j * 512 + 512], xn3T[:], wdT[:, j * 512:j * 512 + 512],
                                   start=True, stop=True)
                mm.then_inc(s["h_ps"], 1)

            f1h = psF[:, 2, :].bitcast(f16)

            def keys_turn(t):
                pe.wait_ge(s["us_ready"], t + 1)
                for h in range(FH):
                    mm = pe.transpose(f1h[:, h * 128:h * 128 + 128], us[:, h, :, :].rearrange("p a b -> p (a b)"),
                                      ident16[:])
                mm.then_inc(s["usT_ps"], 1)

            def sums(h):
                def step(t):
                    if h == 0:
                        pe.wait_ge(s["usT_sb"], t + 1)
                        pe.wait_ge(s["gelu_done"], t + 1)
                    elif h >= 2:
                        pe.wait_ge(s["mw_done"], FH * t + h - 1)
                    for j in range(2):
                        mm = pe.matmul(fslot[h % 2][:, j * 512:j * 512 + 512], usT[:, h, :],
                                       sel[:, j * 512:j * 512 + 512], start=True, stop=True)
                    mm.then_inc(s["s_ps"], 1)
                return step

            def g_turn(t):
                pe.wait_ge(s["g_ready"], t + 1)
                for c in range(EC):
                    mm = pe.transpose(f0[:, c * 128:c * 128 + 128], g[:, c * 128:c * 128 + 128], ident[:])
                mm.then_inc(s["gT_ps"], 1)

            def experts_out(t):
                pe.wait_ge(s["gT_sb"], t + 1)
                for c in range(EC):
                    mm = pe.matmul(f1[:, 0:D], gT[:, c, :], wup[:, c, :], start=(c == 0), stop=(c == EC - 1))
                mm.then_inc(s["y_ps"], 1)

            attention = [xn_turn, queries(0), queries(1), scores(0), scores(1), probs_turn(0), probs_turn(1),
                         mix(0), mix(1), cross_out, xn2_turn, paths_values, feat_turn, similarity, tree_mix,
                         tree_turn, tree_out]
            experts = [xn3_turn, key_scores, hidden, keys_turn] + [sums(h) for h in range(FH)] + [g_turn, experts_out]
            run(pe, attention, experts, PE_ORDER, lambda ta, te: None)

        @block.scalar
        def _(act):
            for j in range(4):
                act.wait_ge(s["setup_ps"], j + 1)
                act.activation(qk[:, 4 * j:4 * j + 4, :].rearrange("p (i e) c -> p e i c", e=2),
                               psA[:, 2 * (j % 2):2 * (j % 2) + 2, 0:2 * CD].rearrange("p e (i c) -> p e i c", i=2),
                               ACT.Copy, scale=float(XD) ** -0.5).then_inc(s["setup_sb"], 1)
            for j in range(4):
                act.wait_ge(s["setup_ps"], j + 5)
                act.activation(vo[:, 4 * j:4 * j + 4, :].rearrange("p (i e) c -> p e i c", e=2),
                               psA[0:CD, 2 * (j % 2):2 * (j % 2) + 2, 0:2 * D].rearrange("p e (i c) -> p e i c", i=2),
                               ACT.Copy).then_inc(s["setup_sb"], 1)
            act.wait_ge(s["setup_ps"], 9)
            act.activation(fqk[:], f0[:, 0:512], ACT.Copy).then_inc(s["setup_sb"], 1)
            act.wait_ge(s["setup_ps"], 10)
            act.activation(fbk[:], f1[0:1, 0:512], ACT.Copy).then_inc(s["setup_sb"], 1)

            def copy_step(waits, out, in_, signal, scale=None):
                def step(t):
                    for name, per, k in waits:
                        act.wait_ge(s[name], t * per + k)
                    if scale is None:
                        act.activation(out, in_, ACT.Copy).then_inc(s[signal], 1)
                    else:
                        act.activation(out, in_, ACT.Identity, scale=scale, bias=0.0).then_inc(s[signal], 1)
                return step

            take_xnT = copy_step([("xnT_ps", 1, 1)], xnT[:], a0[:, 0:128], "xnT_sb")
            take_tT = copy_step([("tT_ps", 2, 1)], tT[:, :, 0:8, :].rearrange("c b h q -> c h b q"),
                                a1[0:CD, :].rearrange("c (h b q) -> c h b q", h=8, b=2), "tT0_sb")

            def exps(b):
                def step(t):
                    act.wait_ge(s["max_done"], 2 * t + 1 + b)
                    for k in range(XHP):
                        ins = act.activation(p[:, b, k, :], aslot[1 - b][:, k * M:k * M + M], ACT.Exp,
                                             bias=negmax[:, b, k:k + 1], accum_out=rowsum[:, b, k:k + 1])
                    ins.then_inc(s["exp_done"], 1)
                return step

            def take_pT(b):
                return copy_step([("pT_ps", 2, 1 + b)], pT[:, b, :], aslot[1 - b][:, :], "pT_sb")

            def take_u(b):
                return copy_step([("u_ps", 2, 1 + b)], uT[:, :, b, :],
                                 aslot[1 - b][0:CD, :].rearrange("c (h q) -> c h q", h=XH), f"u{b}_sb")

            take_xn2T = copy_step([("xn2T_ps", 1, 1)], xn2T[:], a0[:, 0:128], "xn2T_sb")

            def alphas(t):
                act.wait_ge(s["pv_ps"], t + 1)
                act.activation(alpha[:].rearrange("p h d -> p (h d)"), a1[:, 0:AH * DEPTH], ACT.Tanh,
                               scale=0.5).then_inc(s["alpha_done"], 1)
                for b in range(2):
                    act.activation(vblk[N * b:N * b + N, :, b, 0:AD],
                                   a1[N * b:N * b + N, 128:256].rearrange("p (h d) -> p h d", h=AH),
                                   ACT.Copy).then_inc(s["v_sb"], 1)

            take_featT = copy_step([("featT_ps", 1, 1)], featT[:].rearrange("p c t -> p (c t)"), a0[:, 0:512],
                                   "featT_sb", scale=rootc[:, 0:1])

            def tree_exp(t):
                act.wait_ge(s["sim_ps"], t + 1)
                act.activation(ap_[:].rearrange("p r c q -> p r (c q)"), psA[:, :, 0:256], ACT.Exp)\
                   .then_inc(s["sime"], 1)

            take_actxT = copy_step([("actxT_ps", 1, 1)], actxT[:], a1[:, 0:128], "actxT_sb")
            take_xn3T = copy_step([("xn3T_ps", 1, 1)], xn3T[:], f0[:, 0:128], "xn3T_sb")

            def gelu(t):
                act.wait_ge(s["h_ps"], t + 1)
                act.activation(gh[:], f0[:, :], ACT.Gelu).then_inc(s["gelu_done"], 1)

            take_usT = copy_step([("usT_ps", 1, 1)], usT[:].rearrange("p h t -> p (h t)"),
                                 psF[:, 2, :].bitcast(f16), "usT_sb")

            def exp_best(t):
                act.wait_ge(s["best_ready"], t + 1)
                act.activation(ebest[:], best[:, :, 0:TOPK], ACT.Exp).then_inc(s["ebest_done"], 1)

            def exp_sums(h):
                def step(t):
                    act.wait_ge(s["s_ps"], FH * t + h + 1)
                    wait_past(act, s["mw_done"], FH * t + max(h - 1, 0))
                    act.activation(ew[:, h % 2, :], fslot[h % 2][:, :], ACT.Exp).then_inc(s["ew_done"], 1)
                return step

            take_gT = copy_step([("gT_ps", 1, 1)], gT[:].rearrange("p c t -> p (c t)"), f0[:, :], "gT_sb")

            attention = [take_xnT, take_tT, exps(0), exps(1), take_pT(0), take_pT(1), take_u(0), take_u(1),
                         take_xn2T, alphas, take_featT, tree_exp, take_actxT]
            experts = [take_xn3T, gelu, take_usT, exp_best] + [exp_sums(h) for h in range(FH)] + [take_gT]
            run(act, attention, experts, ACT_ORDER, lambda ta, te: None)

        @block.vector
        def _(dve):
            dve.memset(ones[:], 1.0).then_inc(s["consts"], 1)

            class Links:
                def __init__(self, sm, per_tile):
                    self.sm, self.per_tile = sm, per_tile

                def begin(self, t):
                    if t is not None:
                        self.base, self.n = t * self.per_tile, 0

                def done(self, ins):
                    ins.then_inc(self.sm, 1)
                    self.n += 1

                def wait(self):
                    dve.wait_ge(self.sm, self.base + self.n)

                def wait_apart(self):
                    self.wait()
                    dve.nop(nofuse=True)

                def end(self):
                    assert self.n == self.per_tile, self.n

            la = Links(s["dve_x"], DVE_A)
            le = Links(s["dve_f"], DVE_E)

            def norm_steps(src, st_, mv_, rs_, out, name_v, name_r, name_o):
                def stats(t):
                    la.done(dve.bn_stats(st_[:], src))
                    la.wait_apart()
                    la.done(dve.bn_aggr(mv_[:], st_[:]))
                    la.wait()
                    dve.tensor_scalar_add(mv_[:, 1:2], mv_[:, 1:2], 1e-5).then_inc(s[name_v], 1)

                def apply(t):
                    dve.wait_ge(s[name_r], t + 1)
                    dve.tensor_scalar(out[:], src, mv_[:, 0:1], rs_[:, 0:1], ALU.subtract, ALU.mult)\
                       .then_inc(s[name_o], 1)
                return stats, apply

            n1 = norm_steps(x[:], st, mv, rstd, xn, "var1", "rstd1", "xn_ready")
            n2 = norm_steps(x2[:], st2, mv2, rstd2, xn2, "var2", "rstd2_s", "xn2_ready")
            n3 = norm_steps(x3[:], st3, mv3, rstd3, xn3, "var3", "rstd3_s", "xn3_ready")

            def norm1(t):
                dve.wait_ge(s["x_in"], 16 * (t + 1))
                n1[0](t)
                n1[1](t)

            def take_tT(t):
                dve.wait_ge(s["tT_ps"], 2 * t + 2)
                dve.tensor_copy(tT[:, :, 8:16, :].rearrange("c b h q -> c h b q"),
                                a0[0:CD, :].rearrange("c (h b q) -> c h b q", h=8, b=2)).then_inc(s["tT1_sb"], 1)

            def maxes(b):
                def step(t):
                    dve.wait_ge(s["sc_ps"], 2 * t + 1 + b)
                    dve.tensor_reduce(negmax[:, b, :], aslot[1 - b][:, :].rearrange("p (k m) -> p k m", k=XHP),
                                      AX.X, ALU.max, negate=True).then_inc(s["max_done"], 1)
                return step

            def rrows(b):
                def step(t):
                    dve.wait_ge(s["exp_done"], 2 * t + 1 + b)
                    dve.reciprocal(rrow[:, b, :], rowsum[:, b, :]).then_inc(s["rrow_done"], 1)
                return step

            def add_cross(t):
                dve.wait_ge(s["xo_ps"], t + 1)
                dve.tensor_tensor(x2[:], x[:], a1[:, 0:D], ALU.add).then_inc(s["x2_ready"], 1)
                dve.wait_ge(s["x2_ready"], t + 1)
                n2[0](t)
                n2[1](t)

            def tree_norm(t):
                dve.wait_ge(s["actx_ps"], t + 1)
                m = a0[0:N, 0:AH * 18].rearrange("q (h b d) -> q h b d", h=AH, b=2)
                la.done(dve.reciprocal(arz[:], m[:, :, :, AD]))
                la.wait()
                for b in range(2):
                    ins = dve.tensor_tensor(actx[:, b, :].rearrange("q (h d) -> q h d", h=AH), m[:, :, b, 0:AD],
                                            arz[:, :, b].unsqueeze(2).to_broadcast([N, AH, AD]), ALU.mult)
                ins.then_inc(s["actx_ready"], 1)

            def add_tree(t):
                wait_past(dve, s["y_ready"], t)
                dve.wait_ge(s["ao_ps"], t + 1)
                la.done(dve.tensor_tensor(x3[:], x2[:], a0[:, 0:D], ALU.add))
                la.wait()
                n3[0](t)
                n3[1](t)

            f1k = f1[:, 0:512].rearrange("p (k i) -> p k i", k=NQ)

            def key_tops(t):
                dve.wait_ge(s["key_ps"], t + 1)
                dve.nop(nofuse=True)
                for k in range(NQ):
                    ins = dve.max(top[:, k, 0:8], f1k[:, k, :])
                le.done(ins)
                le.wait()
                le.done(dve.tensor_tensor(u[:], f1k, top[:, :, 0:1].to_broadcast([128, NQ, NSQ]), ALU.subtract))
                le.wait()
                le.done(dve.tensor_scalar_max(u[:], u[:], FLOOR))
                le.wait_apart()
                for k in range(NQ):
                    ins = dve.max(tops[:, k, 0:8], u[:, k, :])
                uh = u[:].rearrange("p (h e) i -> p h (e i)", h=FH)
                le.done(dve.tensor_copy(us[:, :, 0, :], uh))
                le.wait()
                dve.tensor_tensor(us[:, :, 1, :], uh, us[:, :, 0, :], ALU.subtract).then_inc(s["us_ready"], 1)

            def key_tops2(t):
                le.wait_apart()
                for k in range(NQ):
                    ins = dve.match_replace(u2[:, k, :], tops[:, k, 0:8], u[:, k, :], DROPPED)
                le.done(ins)
                le.wait_apart()
                for k in range(NQ):
                    ins = dve.max(tops[:, k, 8:16], u2[:, k, :])
                le.done(ins)

            def candidates(t):
                le.wait()
                tv = tops[:].rearrange("p (h e) r -> p h e r", e=2)
                at, i = 0, 0
                while i <= TOPK:
                    w = CAND[i]
                    n = CAND.count(w)
                    shape = [128, FH, n, w]
                    dst = cand[:, :, at:at + n * w].rearrange("p h (n w) -> p h n w", n=n)
                    le.done(dve.tensor_tensor(dst, tv[:, :, 0, i:i + n].unsqueeze(3).to_broadcast(shape),
                                              tv[:, :, 1, 0:w].unsqueeze(2).to_broadcast(shape), ALU.add))
                    at += n * w
                    i += n
                le.wait_apart()
                for h in range(FH):
                    ins = dve.max(best[:, h, 0:8], cand[:, h, :])
                le.done(ins)
                le.wait_apart()
                for h in range(FH):
                    ins = dve.match_replace(cand2[:, h, :], best[:, h, 0:8], cand[:, h, :], DROPPED)
                le.done(ins)
                le.wait_apart()
                for h in range(FH):
                    ins = dve.max(best[:, h, 8:16], cand2[:, h, :])
                ins.then_inc(s["best_ready"], 1)
                dve.wait_ge(s["best_ready"], t + 1)
                le.done(dve.tensor_tensor(cut[:], best[:, :, TOPK - 1], best[:, :, TOPK], ALU.add))
                le.wait()
                le.done(dve.tensor_scalar_mul(cut[:], cut[:], 0.5))
                dve.wait_ge(s["ebest_done"], t + 1)
                le.done(dve.reduce_sum(z[:], ebest[:], AX.X))
                le.wait()
                le.done(dve.reciprocal(rz[:], z[:]))
                le.wait()

            def mask_sum(h):
                def step(t):
                    dve.wait_ge(s["ew_done"], FH * t + h + 1)
                    dve.scalar_tensor_tensor(out=mw[:, h % 2, :], in0=fslot[h % 2][:, :], scalar=cut[:, h:h + 1],
                                             in1=ew[:, h % 2, :], op0=ALU.is_ge, op1=ALU.mult)\
                       .then_inc(s["mw_done"], 1)
                    dve.wait_ge(s["mw_done"], FH * t + h + 1)
                    if h == 0:
                        wait_past(dve, s["g_ready"], t)
                        ins = dve.tensor_scalar_mul(wsum[:], mw[:, 0, :], rz[:, 0:1])
                    else:
                        ins = dve.scalar_tensor_tensor(out=wsum[:], in0=mw[:, h % 2, :], scalar=rz[:, h:h + 1],
                                                       in1=wsum[:], op0=ALU.mult, op1=ALU.add)
                    if h < FH - 1:
                        le.done(ins)
                        le.wait()
                    else:
                        ins.then_inc(s["wsum_ready"], 1)
                return step

            def add_experts(t):
                dve.wait_ge(s["y_ps"], t + 1)
                wait_past(dve, s["out_done"], 16 * t)
                dve.tensor_tensor(y[:], x3[:], f1[:, 0:D], ALU.add).then_inc(s["y_ready"], 1)

            attention = [norm1, take_tT, maxes(0), maxes(1), rrows(0), rrows(1), add_cross, tree_norm, add_tree]
            experts = [key_tops, key_tops2, candidates] + [mask_sum(h) for h in range(FH)] + [add_experts]

            def begin(ta, te):
                la.begin(ta)
                le.begin(te)
            run(dve, attention, experts, DVE_ORDER, begin)
            le.end()
            la.end()

        @block.gpsimd
        def _(pool):
            pool.memset(halfneg[:], -0.5).then_inc(s["pool_x"], 1)
            pool.memset(feat[:, :, 0:1], 1.0).then_inc(s["pool_x"], 1)
            pool.memset(vblk[:], 0.0).then_inc(s["pool_x"], 1)
            pool.wait_ge(s["pool_x"], 3)
            for b in range(2):
                pool.memset(vblk[N * b:N * b + N, :, b, AD:AD + 1], 1.0).then_inc(s["pool_x"], 1)
            pool.wait_ge(s["pool_x"], 5)
            pool.wait_ge(s["wload"], 16 * len(WEIGHTS))

            def root(name_v, mv_, rs_, name_r):
                def step(t):
                    pool.wait_ge(s[name_v], t + 1)
                    pool.tensor_tensor(rs_[:], mv_[:, 1:2], halfneg[:], ALU.pow).then_inc(s[name_r], 1)
                return step

            def norm(b):
                def step(t):
                    pool.wait_ge(s["rrow_done"], 2 * t + 1 + b)
                    pool.tensor_tensor(p[:, b, :, :], p[:, b, :, :],
                                       rrow[:, b, :].unsqueeze(2).to_broadcast([128, XHP, M]), ALU.mult)\
                        .then_inc(s["norm_done"], 1)
                return step

            def features(t):
                pool.wait_ge(s["alpha_done"], t + 1)
                for l in range(DEPTH):
                    w = 2 ** l
                    ins = pool.tensor_tensor(feat[:, :, w:2 * w], feat[:, :, 0:w],
                                             alpha[:, :, l:l + 1].to_broadcast([128, AH, w]), ALU.mult)
                    if l < DEPTH - 1:
                        ins.then_inc(s["pool_x"], 1)
                        pool.wait_ge(s["pool_x"], 5 + (DEPTH - 1) * t + l + 1)
                ins.then_inc(s["feat_ready"], 1)

            def causal(t):
                pool.wait_ge(s["sime"], t + 1)
                pool.wait_ge(s["v_sb"], 2 * t + 2)
                pool.tensor_tensor(am[:].rearrange("p r c q -> p (r c) q"), ap_[:].rearrange("p r c q -> p (r c) q"),
                                   cmask[:].unsqueeze(1).to_broadcast([128, AH, N]), ALU.mult)\
                    .then_inc(s["am_done"], 1)

            def gate(t):
                pool.wait_ge(s["wsum_ready"], t + 1)
                pool.wait_ge(s["gelu_done"], t + 1)
                pool.tensor_tensor(g[:], wsum[:], gh[:], ALU.mult).then_inc(s["g_ready"], 1)

            attention = [root("var1", mv, rstd, "rstd1"), norm(0), norm(1), root("var2", mv2, rstd2, "rstd2_s"),
                         features, causal, root("var3", mv3, rstd3, "rstd3_s")]
            run(pool, attention, [gate], POOL_ORDER, lambda ta, te: None)


DVE_A = 8
DVE_E = 24
PE_ORDER = "e" "a" "e" "a" "e" "a" "a" "a" "e" "a" "e" "a" "e" "a" "e" "a" "e" "a" "e" "a" "e" "a" "e" "a" "e" "a" "a" "a" "e" "e" "a"
ACT_ORDER = "e" "a" "a" "e" "a" "a" "e" "e" "e" "a" "e" "a" "e" "a" "e" "a" "e" "a" "e" "a" "e" "a" "e" "a" "a" "e"
DVE_ORDER = "a" "e" "a" "a" "a" "e" "a" "a" "e" "eeeee" "a" "eee" "a" "e" "a"
POOL_ORDER = "aaaaaaea"[0:8]


def kernel(**inputs):
    import concourse.bacc as bacc
    from concourse.bass_utils import run_bass_kernel_spmd

    w = {k: np.asarray(v) for k, v in inputs.items()}
    cc = np.ascontiguousarray
    keys = np.zeros((128, 4, 2 * NSQ), np.float32)
    for i in range(4):
        keys[32 * i:32 * i + DQH, i, 0:NSQ] = w["L0_ffn_K1"].T
        keys[32 * i + DQH:32 * i + 2 * DQH, i, NSQ:] = w["L0_ffn_K2"].T
    pair = np.arange(NE)
    one = np.concatenate([np.arange(NSQ)[:, None] == pair // NSQ, np.arange(NSQ)[:, None] == pair % NSQ])
    last = np.array([0] + [f.bit_length() for f in range(1, NF)])
    weight = np.array([sum(2.0 ** -d for d in range(max(l, 1), DEPTH + 1)) for l in last]) / DEPTH
    arrays = {
        "x": cc(w["x"].reshape(B * N, D)), "c": cc(w["ctx_768"]), "cT": cc(w["ctx_768"].transpose(0, 2, 1)),
        "ident": np.eye(128, dtype=np.float32), "ident16": np.eye(128, dtype=np.float16),
        "sel": np.concatenate([one, one]).astype(np.float16),
        "cmask": (np.arange(N)[None, :] >= (np.arange(128) % N)[:, None]).astype(np.float32),
        "rootc": np.tile(np.sqrt(weight), 4).astype(np.float32)[:, None],
        "wqT": cc(w["L0_xattn_Wq"].T), "wkT": cc(w["L0_xattn_Wk"].T), "wvT": cc(w["L0_xattn_Wv"].T),
        "wo": cc(w["L0_xattn_Wo"]), "bo": w["L0_xattn_bo"][None, :],
        "wp": w["L0_attn_Wp"], "bp": w["L0_attn_bp"][None, :], "awv": w["L0_attn_Wv"], "awo": w["L0_attn_Wo"],
        "fwqT": cc(w["L0_ffn_Wq"].T), "fbqT": cc(w["L0_ffn_bq"].reshape(2, 128).T), "keys": keys,
        "wdT": cc(w["L0_ffn_W_down"][0:NE].T), "wup": cc(w["L0_ffn_W_up"][0:NE]),
    }
    nc = bacc.Bacc("TRN2", target_bir_lowering=False, num_devices=1)
    aps = {k: nc.dram_tensor(k + "_dram", v.shape, mybir.dt.from_np(v.dtype), kind="ExternalInput").ap()
           for k, v in arrays.items()}
    aps["y"] = nc.dram_tensor("y_dram", (B * N, D), mybir.dt.float32, kind="ExternalOutput").ap()
    build(nc, aps)
    r = run_bass_kernel_spmd(nc, [{k + "_dram": v for k, v in arrays.items()}], core_ids=[0])
    return r.results[0]["y_dram"].reshape(B, N, D)
```

```python
from contextlib import ExitStack

import numpy as np
import concourse.bass as bass
from concourse import mybir

B, N, D = 64, 64, 128
M, CD = 128, 96
XH, XD = 16, 64
AH, DEPTH, AD = 16, 5, 8
NF = 2 ** DEPTH
FH, NSQ, TOPK, DQH = 8, 32, 10, 16
NE = NSQ * NSQ
PAIR = 2 * N
NT = B * N // PAIR
XHP, AHP = XH // 2, AH // 2
EC = NE // 128
NQ = 2 * FH
DROPPED = -3.0e38
NMW = 4
FLOOR = -30000.0

CAND = [(TOPK + 1) // (i + 1) for i in range(TOPK + 1)]
NCAND = sum(CAND)


def build(nc, a):
    f32, f16 = mybir.dt.float32, mybir.dt.float16
    ALU, ACT, AX = mybir.AluOpType, mybir.ActivationFunctionType, mybir.AxisListType
    ctx = ExitStack()
    with ctx:
        def sb(name, shape, dt=f32):
            return ctx.enter_context(nc.sbuf_tensor(name, shape, dt))

        def sem(name):
            return ctx.enter_context(nc.semaphore(name))

        ident = sb("ident", [128, 128])
        ident16 = sb("ident16", [128, 128], f16)
        sel = sb("sel", [128, NE], f16)
        cmask = sb("cmask", [128, N])
        rootc = sb("rootc", [2 * NF, 1])
        ones = sb("ones", [1, 128])
        halfneg = sb("halfneg", [128, 1])
        wqT = sb("wqT", [128, XHP, D])
        wkT = sb("wkT", [128, XHP, CD])
        wvT = sb("wvT", [128, XHP, CD])
        wo = sb("wo", [128, XHP, D])
        bo = sb("bo", [1, D])
        wp = sb("wp", [D, AH * DEPTH])
        bp = sb("bp", [1, AH * DEPTH])
        awv = sb("awv", [D, D])
        awo = sb("awo", [D, D])
        fwqT = sb("fwqT", [128, 2, D])
        fbqT = sb("fbqT", [128, 2])
        keys = sb("keys", [128, 4, 2 * NSQ])
        wdT = sb("wdT", [D, NE])
        wup = sb("wup", [128, EC, D])
        qk = sb("qk", [D, XH, CD])
        vo = sb("vo", [CD, XH, D])
        fqk = sb("fqk", [D, FH * 2 * NSQ])
        fbk = sb("fbk", [1, FH * 2 * NSQ])
        x = sb("x", [128, D])
        c0 = sb("c0", [M, 2, CD])
        cT = sb("cT", [CD, 2, M])
        st = sb("st", [128, 6])
        mv = sb("mv", [128, 2])
        rstd = sb("rstd", [128, 1])
        xn = sb("xn", [128, D])
        xnT = sb("xnT", [D, 128])
        q = sb("q", [CD, 2, XH, N])
        negmax = sb("negmax", [128, 4, 4])
        rowsum = sb("rowsum", [128, 4, 4])
        rrow = sb("rrow", [128, 4, 4])
        p = sb("p", [128, 4, 4, M])
        pT = sb("pT", [M, 4, 8 * N])
        uT = sb("uT", [CD, XH, 2, N])
        x2 = sb("x2", [128, D])
        st2 = sb("st2", [128, 6])
        mv2 = sb("mv2", [128, 2])
        rstd2 = sb("rstd2", [128, 1])
        xn2 = sb("xn2", [128, D])
        xn2T = sb("xn2T", [D, 128])
        alpha = sb("alpha", [128, AH, DEPTH])
        feat = sb("feat", [128, AH, NF])
        featT = sb("featT", [2 * NF, AHP, 128])
        vblk = sb("vblk", [128, AH, 2, AD + 1])
        ap_ = sb("ap_", [128, 2, AHP, N])
        am = sb("am", [128, 2, AHP, N])
        arz = sb("arz", [N, AH, 2])
        actx = sb("actx", [N, 2, AH * AD])
        actxT = sb("actxT", [D, 128])
        x3 = sb("x3", [128, D])
        st3 = sb("st3", [128, 6])
        mv3 = sb("mv3", [128, 2])
        rstd3 = sb("rstd3", [128, 1])
        xn3 = sb("xn3", [128, D])
        xn3T = sb("xn3T", [D, 128])
        top = sb("top", [128, NQ, 8])
        tops = sb("tops", [128, NQ, 16])
        u = sb("u", [128, NQ, NSQ])
        u2 = sb("u2", [128, NQ, NSQ])
        lnz = sb("lnz", [128, FH])
        x3b = sb("x3b", [128, D])
        xn3K = sb("xn3K", [D, 128])
        usK = sb("usK", [128, FH, 128], f16)
        lnzE = sb("lnzE", [128, FH])
        cutE = sb("cutE", [128, FH])
        x3c = sb("x3c", [128, D])
        xr = sb("xr", [128, D])
        us = sb("us", [128, FH, 2, 2 * NSQ], f16)
        usT = sb("usT", [128, FH, 128], f16)
        cand = sb("cand", [128, FH, NCAND])
        cand2 = sb("cand2", [128, FH, NCAND])
        best = sb("best", [128, FH, 16])
        cut = sb("cut", [128, FH])
        ebest = sb("ebest", [128, FH, TOPK])
        z = sb("z", [128, FH])
        rz = sb("rz", [128, FH])
        gh = sb("gh", [128, NE])
        ew = sb("ew", [128, 2, NE])
        mw = sb("mw", [128, NMW, NE])
        wsum = sb("wsum", [128, NE])
        g = sb("g", [128, NE])
        gT = sb("gT", [128, EC, 128])
        y = sb("y", [128, D])

        psX = ctx.enter_context(nc.psum_tensor("psX", [128, 2, 512], f32))
        psT = ctx.enter_context(nc.psum_tensor("psT", [128, 2, 512], f32))
        psF = ctx.enter_context(nc.psum_tensor("psF", [128, 4, 512], f32))
        x0, x1 = psX[:, 0, :], psX[:, 1, :]
        t0, t1 = psT[:, 0, :], psT[:, 1, :]
        t01 = psT[:].rearrange("p a b -> p (a b)")
        t1h = t1.bitcast(f16)
        f0 = psF[:, 0:2, :].rearrange("p a b -> p (a b)")
        f1 = psF[:, 2:4, :].rearrange("p a b -> p (a b)")
        xbank = [x0, x1]
        sslot = [f1, f0]

        names = """wload ones_set setup_ps setup_sb x_in xr_in c_in cT_in out_done
            dve_x dve_y dve_t dve_k pool_set pool_t
            var1 root1 xn_ready xnT_ps xnT_sb q_ps qa_sb qd_sb
            sc_ps max_done exp_done rrow_done norm_done pT_ps pT_sb u_ps u_sb xo_ps x2_ready
            var2 root2 xn2_ready xn2T_ps xn2T_sb pv_ps expz_done alpha_done v_sb feat_ready featT_ps featT_sb
            sim_ps sime am_done actx_ps actx_ready actxT_ps actxT_sb ao_ps x3_ready var3 root3 xn3_ready
            xn3T_ps xn3T_sb key_ps us_ready usT_ps usT_sb best_ready ebest_done rz_ready lnz_ready usE_ready
            x3b_ready x3c_ready h_ps gelu_done s_ps ew_done mw_done wsum_step g_ready gT_ps gT_sb y_ps y_ready""".split()
        s = {n: sem(n) for n in names}
        block = ctx.enter_context(nc.Block())

        WEIGHTS = [(wqT, a["wqT"].rearrange("(c p) d -> p c d", p=128)),
                   (wkT, a["wkT"].rearrange("(c p) d -> p c d", p=128)),
                   (wvT, a["wvT"].rearrange("(c p) d -> p c d", p=128)),
                   (wo, a["wo"].rearrange("(c p) d -> p c d", p=128)),
                   (fwqT, a["fwqT"].rearrange("(c p) d -> p c d", p=128)),
                   (fbqT, a["fbqT"]), (keys, a["keys"]),
                   (ident, a["ident"]), (bo, a["bo"]), (wp, a["wp"]), (bp, a["bp"]), (awv, a["awv"]),
                   (awo, a["awo"]), (rootc, a["rootc"]), (cmask, a["cmask"]),
                   (ident16, a["ident16"]), (sel, a["sel"]), (wdT, a["wdT"]),
                   (wup, a["wup"].rearrange("(c p) d -> p c d", p=128))]
        xt = a["x"].rearrange("(t p) d -> t p d", p=128)
        ct = a["c"].rearrange("(t b) m c -> t m b c", b=2)
        ctT = a["cT"].rearrange("(t b) c m -> t c b m", b=2)
        yt = a["y"].rearrange("(t p) d -> t p d", p=128)

        def run(eng, steps, order, begin=None):
            assert sorted(order) == sorted(steps), set(order) ^ set(steps)
            lag = {"x": 0, "y": 1, "t": 1, "k": 2, "e": 3}

            def turn(t, stages):
                if begin:
                    for st in stages:
                        begin(st, t - lag[st])
                for name in order:
                    if name[0] in stages:
                        steps[name](t - lag[name[0]])

            turn(0, "x")
            turn(1, "xyt")
            turn(2, "xytk")
            turn(3, "xytke")
            with eng.Fori(4, NT) as t:
                turn(t, "xytke")
            turn(NT, "ytke")
            turn(NT + 1, "ke")
            turn(NT + 2, "e")

        def wait_past(eng, sm, count):
            if not (isinstance(count, int) and count <= 0):
                eng.wait_ge(sm, count)

        @block.sync
        def _(sp):
            def after(name, count):
                sp.wait_ge(s[name], count)
                sp.nop(nofuse=True)

            def load_scores(t):
                if not isinstance(t, int) or t > 0:
                    after("xn_ready", t)
                sp.dma_start(x[:], xt[t]).then_inc(s["x_in"], 16)
                if not isinstance(t, int) or t > 0:
                    after("sc_ps", 4 * t)
                sp.dma_start(cT[:], ctT[t]).then_inc(s["cT_in"], 16)

            def load_mix(t):
                if not isinstance(t, int) or t > 0:
                    after("u_ps", 4 * t)
                sp.dma_start(c0[:], ct[t]).then_inc(s["c_in"], 16)
                if not isinstance(t, int) or t > 0:
                    after("x2_ready", t)
                sp.dma_start(xr[:], xt[t]).then_inc(s["xr_in"], 16)

            def store(t):
                after("y_ready", t + 1)
                sp.dma_start(yt[t], y[:]).then_inc(s["out_done"], 16)

            for dst, src in WEIGHTS:
                sp.dma_start(dst[:], src).then_inc(s["wload"], 16)
            load_scores(0)
            for t in range(1, 4):
                load_scores(t)
                load_mix(t - 1)
            with sp.Fori(4, NT) as t:
                load_scores(t)
                load_mix(t - 1)
                store(t - 4)
            load_mix(NT - 1)
            for t in range(NT - 4, NT):
                store(t)
            sp.wait_ge(s["out_done"], 16 * NT)

        @block.tensor
        def _(pe):
            pe.wait_ge(s["wload"], 16 * len(WEIGHTS))
            pe.wait_ge(s["ones_set"], 1)

            def setup_round(n, mms):
                if n >= 1:
                    pe.wait_ge(s["setup_sb"], n)
                for out, lhsT, rhs in mms:
                    mm = pe.matmul(out, lhsT, rhs, start=True, stop=True)
                mm.then_inc(s["setup_ps"], 1)

            for n, (lw, rw, w, rows) in enumerate(((wqT, wkT, CD, D), (wvT, wo, D, CD))):
                for j in range(4):
                    mms = []
                    for i in range(4):
                        h = 4 * j + i
                        r = XD * (h % 2)
                        mms.append((psF[0:rows, h % 2 + 2 * (j % 2), (i // 2) * w:(i // 2 + 1) * w],
                                    lw[r:r + XD, h // 2, :], rw[r:r + XD, h // 2, :]))
                    setup_round(4 * n + j, mms)
            kflat = keys[:].rearrange("p g i -> p (g i)")
            setup_round(8, [(x0[:, 256 * c:256 * c + 256], fwqT[:, c, :], kflat) for c in range(2)])
            setup_round(9, [(x1[0:1, 256 * c:256 * c + 256], fbqT[:, c:c + 1], kflat) for c in range(2)])
            pe.wait_ge(s["setup_sb"], 10)

            steps = {}

            def x_turn(t):
                pe.wait_ge(s["xn_ready"], t + 1)
                wait_past(pe, s["u_sb"], 4 * t)
                pe.transpose(x0[:, 0:128], xn[:], ident[:]).then_inc(s["xnT_ps"], 1)
            steps["x.turn"] = x_turn

            def queries(k):
                def step(t):
                    if k == 0:
                        pe.wait_ge(s["xnT_sb"], t + 1)
                        wait_past(pe, s["x2_ready"], t)
                    elif k == 2:
                        pe.wait_ge(s["qa_sb"], 2 * t + 1)
                    elif k == 3:
                        pe.wait_ge(s["qd_sb"], 2 * t + 1)
                    for i in range(4):
                        mm = pe.matmul(xbank[1 - k % 2][0:CD, i * 128:i * 128 + 128], qk[:, 4 * k + i, :],
                                       xnT[:], start=True, stop=True)
                    mm.then_inc(s["q_ps"], 1)
                return step

            def scores(k):
                def step(t):
                    pe.wait_ge(s["cT_in"], 16 * (t + 1))
                    if k < 2:
                        pe.wait_ge(s["qa_sb"], 2 * t + 2)
                        pe.wait_ge(s["qd_sb"], 2 * t + 2)
                    else:
                        pe.wait_ge(s["exp_done"], 4 * t + k - 1)
                    b = k // 2
                    for i in range(4):
                        h = 8 * (k % 2) + 2 * i
                        mm = pe.matmul(xbank[1 - k % 2][:, i * M:i * M + M],
                                       q[:, b, h:h + 2, :].rearrange("c h q -> c (h q)"),
                                       cT[:, b, :], start=True, stop=True)
                    mm.then_inc(s["sc_ps"], 1)
                return step

            def probs_turn(k):
                def step(t):
                    if k < 2:
                        pe.wait_ge(s["exp_done"], 4 * t + k + 3)
                    else:
                        pe.wait_ge(s["pT_sb"], 4 * t + k - 1)
                    pe.wait_ge(s["norm_done"], 4 * t + k + 1)
                    for i in range(4):
                        mm = pe.transpose(xbank[1 - k % 2][:, i * 128:i * 128 + 128], p[:, k, i, :], ident[:])
                    mm.then_inc(s["pT_ps"], 1)
                return step

            def mix(k):
                def step(t):
                    pe.wait_ge(s["c_in"], 16 * (t + 1))
                    if k < 2:
                        pe.wait_ge(s["pT_sb"], 4 * t + k + 3)
                    else:
                        pe.wait_ge(s["u_sb"], 4 * t + k - 1)
                    pe.matmul(xbank[1 - k % 2][0:CD, :], c0[:, k // 2, :], pT[:, k, :],
                              start=True, stop=True).then_inc(s["u_ps"], 1)
                return step

            for k in range(4):
                steps[f"x.q{k}"], steps[f"x.s{k}"] = queries(k), scores(k)
                steps[f"x.p{k}"], steps[f"y.m{k}"] = probs_turn(k), mix(k)

            def cross_out(t):
                pe.wait_ge(s["u_sb"], 4 * t + 4)
                pe.matmul(x1[:, 0:D], ones[:], bo[:], start=True, stop=False)
                for h in range(XH):
                    mm = pe.matmul(x1[:, 0:D], uT[:, h, :, :].rearrange("c b q -> c (b q)"), vo[:, h, :],
                                   start=False, stop=(h == XH - 1))
                mm.then_inc(s["xo_ps"], 1)
            steps["y.out"] = cross_out

            def t_turn(t):
                pe.wait_ge(s["xn2_ready"], t + 1)
                wait_past(pe, s["us_ready"], t)
                pe.transpose(t0[:, 0:128], xn2[:], ident[:]).then_inc(s["xn2T_ps"], 1)
            steps["t.turn"] = t_turn

            def paths_values(t):
                pe.wait_ge(s["xn2T_sb"], t + 1)
                wait_past(pe, s["usT_sb"], t)
                pe.matmul(t1[:, 0:AH * DEPTH], ones[:], bp[:], start=True, stop=False)
                pe.matmul(t1[:, 0:AH * DEPTH], xn2T[:], wp[:], start=False, stop=True)
                pe.matmul(t1[:, 128:256], xn2T[:], awv[:], start=True, stop=True).then_inc(s["pv_ps"], 1)
            steps["t.pv"] = paths_values

            def feat_turn(t):
                pe.wait_ge(s["feat_ready"], t + 1)
                pe.wait_ge(s["v_sb"], 2 * t + 2)
                pe.nop(nofuse=True)
                ff = feat[:].rearrange("p (c r) f -> p c (r f)", c=AHP)
                for c in range(AHP):
                    mm = pe.transpose(t01[0:2 * NF, c * 128:c * 128 + 128], ff[:, c, :], ident[:])
                mm.then_inc(s["featT_ps"], 1)
            steps["t.feat"] = feat_turn

            def similarity(t):
                pe.wait_ge(s["featT_sb"], t + 1)
                for c in range(AHP):
                    for b in range(2):
                        for r in range(2):
                            ft = featT[NF * r:NF * r + NF, c, N * b:N * b + N]
                            mm = pe.matmul(psT[N * b:N * b + N, r, c * N:c * N + N], ft, ft,
                                           start=True, stop=True, tile_position=(NF * r, N * b))
                mm.then_inc(s["sim_ps"], 1)
            steps["t.sim"] = similarity

            def tree_mix(t):
                pe.wait_ge(s["am_done"], t + 1)
                for h in range(AH):
                    mm = pe.matmul(t0[0:N, h * 18:h * 18 + 18], am[:, h % 2, h // 2, :],
                                   vblk[:, h, :, :].rearrange("p b d -> p (b d)"), start=True, stop=True)
                mm.then_inc(s["actx_ps"], 1)
            steps["t.mix"] = tree_mix

            def tree_turn(t):
                pe.wait_ge(s["actx_ready"], t + 1)
                pe.nop(nofuse=True)
                for b in range(2):
                    mm = pe.transpose(t1[:, b * N:b * N + N], actx[:, b, :], ident[0:N, 0:N])
                mm.then_inc(s["actxT_ps"], 1)
            steps["t.cturn"] = tree_turn

            def tree_out(t):
                pe.wait_ge(s["actxT_sb"], t + 1)
                pe.matmul(t0[:, 0:D], actxT[:], awo[:], start=True, stop=True).then_inc(s["ao_ps"], 1)
            steps["t.out"] = tree_out

            def xn3_turn(t):
                pe.wait_ge(s["xn3_ready"], t + 1)
                pe.transpose(t1[:, 0:128], xn3[:], ident[:]).then_inc(s["xn3T_ps"], 1)
            steps["k.turn3"] = xn3_turn

            def key_scores(t):
                pe.wait_ge(s["xn3T_sb"], t + 1)
                pe.matmul(t0, ones[:], fbk[:], start=True, stop=False)
                pe.matmul(t0, xn3K[:], fqk[:], start=False, stop=True).then_inc(s["key_ps"], 1)
            steps["k.key"] = key_scores

            def keys_turn(t):
                pe.wait_ge(s["us_ready"], t + 1)
                for h in range(FH):
                    mm = pe.transpose(t1h[:, h * 128:h * 128 + 128], us[:, h, :, :].rearrange("p a b -> p (a b)"),
                                      ident16[:])
                mm.then_inc(s["usT_ps"], 1)
            steps["k.kturn"] = keys_turn

            def hidden(t):
                pe.wait_ge(s["usE_ready"], t + 1)
                wait_past(pe, s["y_ready"], t)
                for j in range(2):
                    mm = pe.matmul(f0[:, j * 512:j * 512 + 512], xn3T[:], wdT[:, j * 512:j * 512 + 512],
                                   start=True, stop=True)
                mm.then_inc(s["h_ps"], 1)
            steps["e.hid"] = hidden

            def sums(h):
                def step(t):
                    if h == 0:
                        pe.wait_ge(s["usE_ready"], t + 1)
                        wait_past(pe, s["gT_sb"], t)
                    elif h == 1:
                        pe.wait_ge(s["gelu_done"], t + 1)
                    else:
                        pe.wait_ge(s["mw_done"], FH * t + h - 1)
                    for j in range(2):
                        mm = pe.matmul(sslot[h % 2][:, j * 512:j * 512 + 512], usT[:, h, :],
                                       sel[:, j * 512:j * 512 + 512], start=True, stop=True)
                    mm.then_inc(s["s_ps"], 1)
                return step
            for h in range(FH):
                steps[f"e.s{h}"] = sums(h)

            def g_turn(t):
                pe.wait_ge(s["mw_done"], FH * t + FH)
                pe.wait_ge(s["g_ready"], t + 1)
                for c in range(EC):
                    mm = pe.transpose(f1[:, c * 128:c * 128 + 128], g[:, c * 128:c * 128 + 128], ident[:])
                mm.then_inc(s["gT_ps"], 1)
            steps["e.gturn"] = g_turn

            def experts_out(t):
                pe.wait_ge(s["gT_sb"], t + 1)
                for c in range(EC):
                    mm = pe.matmul(f0[:, 0:D], gT[:, c, :], wup[:, c, :], start=(c == 0), stop=(c == EC - 1))
                mm.then_inc(s["y_ps"], 1)
            steps["e.out"] = experts_out
            run(pe, steps, PE_ORDER)

        @block.scalar
        def _(act):
            for n, (dst, w, rows, scale) in enumerate(((qk, CD, D, float(XD) ** -0.5), (vo, D, CD, 1.0))):
                for j in range(4):
                    act.wait_ge(s["setup_ps"], 4 * n + j + 1)
                    act.activation(dst[:, 4 * j:4 * j + 4, :].rearrange("p (i e) c -> p e i c", e=2),
                                   psF[0:rows, 2 * (j % 2):2 * (j % 2) + 2, 0:2 * w]
                                   .rearrange("p e (i c) -> p e i c", i=2),
                                   ACT.Copy, scale=scale).then_inc(s["setup_sb"], 1)
            act.wait_ge(s["setup_ps"], 9)
            act.activation(fqk[:], x0, ACT.Copy).then_inc(s["setup_sb"], 1)
            act.wait_ge(s["setup_ps"], 10)
            act.activation(fbk[:], x1[0:1, :], ACT.Copy).then_inc(s["setup_sb"], 1)

            steps = {}

            def take(name, out, in_, filled, per, k, signal, scale=None, readers=None):
                def step(t):
                    act.wait_ge(s[filled], t * per + k)
                    if readers:
                        wait_past(act, s[readers[0]], readers[1] * t)
                    if scale is None:
                        act.activation(out, in_, ACT.Copy).then_inc(s[signal], 1)
                    else:
                        act.activation(out, in_, ACT.Identity, scale=scale, bias=0.0).then_inc(s[signal], 1)
                steps[name] = step

            take("x.turn", xnT[:], x0[:, 0:128], "xnT_ps", 1, 1, "xnT_sb")
            for k in (0, 2):
                take(f"x.q{k}", q[:, :, 4 * k:4 * k + 4, :].rearrange("c b h q -> c h b q"),
                     x1[0:CD, :].rearrange("c (h b q) -> c h b q", h=4, b=2), "q_ps", 4, k + 1, "qa_sb")

            def exps(k):
                def step(t):
                    act.wait_ge(s["max_done"], 4 * t + k + 1)
                    for i in range(4):
                        ins = act.activation(p[:, k, i, :], xbank[1 - k % 2][:, i * M:i * M + M], ACT.Exp,
                                             bias=negmax[:, k, i:i + 1], accum_out=rowsum[:, k, i:i + 1])
                    ins.then_inc(s["exp_done"], 1)
                return step
            for k in range(4):
                steps[f"x.e{k}"] = exps(k)
                take(f"x.p{k}", pT[:, k, :], xbank[1 - k % 2], "pT_ps", 4, k + 1, "pT_sb")
                take(f"y.m{k}", uT[:, 8 * (k % 2):8 * (k % 2) + 8, k // 2, :],
                     xbank[1 - k % 2][0:CD, :].rearrange("c (h q) -> c h q", h=8), "u_ps", 4, k + 1, "u_sb")

            take("t.turn", xn2T[:], t0[:, 0:128], "xn2T_ps", 1, 1, "xn2T_sb")

            def alphas(t):
                act.wait_ge(s["pv_ps"], t + 1)
                act.activation(alpha[:].rearrange("p h d -> p (h d)"), t1[:, 0:AH * DEPTH], ACT.Exp,
                               scale=-1.0).then_inc(s["expz_done"], 1)
            steps["t.alpha"] = alphas

            def values(t):
                for b in range(2):
                    act.activation(vblk[N * b:N * b + N, :, b, 0:AD],
                                   t1[N * b:N * b + N, 128:256].rearrange("p (h d) -> p h d", h=AH),
                                   ACT.Copy).then_inc(s["v_sb"], 1)
            steps["t.v"] = values
            take("t.feat", featT[:].rearrange("p c t -> p (c t)"), t01[0:2 * NF, :], "featT_ps", 1, 1, "featT_sb",
                 scale=rootc[:, 0:1])

            def tree_exp(t):
                act.wait_ge(s["sim_ps"], t + 1)
                act.activation(ap_[:].rearrange("p r c q -> p (r c q)"), t01, ACT.Exp).then_inc(s["sime"], 1)
            steps["t.exp"] = tree_exp
            take("t.cturn", actxT[:], t1[:, 0:128], "actxT_ps", 1, 1, "actxT_sb")
            take("k.turn3", xn3K[:], t1[:, 0:128], "xn3T_ps", 1, 1, "xn3T_sb", readers=("usE_ready", 1))
            take("k.kturn", usK[:].rearrange("p h t -> p (h t)"), t1h, "usT_ps", 1, 1, "usT_sb",
                 readers=("usE_ready", 1))

            def exp_best(t):
                act.wait_ge(s["best_ready"], t + 1)
                act.activation(ebest[:], best[:, :, 0:TOPK], ACT.Exp).then_inc(s["ebest_done"], 1)
            steps["k.ebest"] = exp_best

            def ln_z(t):
                act.wait_ge(s["rz_ready"], t + 1)
                wait_past(act, s["usE_ready"], t)
                act.activation(lnz[:], rz[:], ACT.Ln).then_inc(s["lnz_ready"], 1)
            steps["k.lnz"] = ln_z

            def gelu(t):
                act.wait_ge(s["h_ps"], t + 1)
                wait_past(act, s["g_ready"], t)
                act.activation(gh[:], f0[:, :], ACT.Gelu).then_inc(s["gelu_done"], 1)
                act.preload_act_table_set("natural_log_exp_and_others")
            steps["e.gelu"] = gelu

            def exp_sums(h):
                def step(t):
                    act.wait_ge(s["s_ps"], FH * t + h + 1)
                    if h == 0:
                        act.wait_ge(s["usE_ready"], t + 1)
                    wait_past(act, s["mw_done"], FH * t + max(h - 1, 0))
                    act.activation(ew[:, h % 2, :], sslot[h % 2][:, :], ACT.Exp, bias=lnzE[:, h:h + 1])\
                       .then_inc(s["ew_done"], 1)
                return step
            for h in range(FH):
                steps[f"e.e{h}"] = exp_sums(h)
            take("e.gturn", gT[:].rearrange("p c t -> p (c t)"), f1, "gT_ps", 1, 1, "gT_sb")
            run(act, steps, ACT_ORDER)

        @block.vector
        def _(dve):
            dve.memset(ones[:], 1.0).then_inc(s["ones_set"], 1)

            class Links:
                def __init__(self, sm, per_tile):
                    self.sm, self.per_tile = sm, per_tile

                def begin(self, t):
                    self.base, self.n = t * self.per_tile, 0

                def done(self, ins):
                    ins.then_inc(self.sm, 1)
                    self.n += 1

                def wait(self):
                    dve.wait_ge(self.sm, self.base + self.n)

                def wait_apart(self):
                    self.wait()
                    dve.nop(nofuse=True)

            links = {"x": Links(s["dve_x"], 2), "y": Links(s["dve_y"], 2), "t": Links(s["dve_t"], 5), "k": Links(s["dve_k"], 16)}
            lx, ly, lt, lk = links["x"], links["y"], links["t"], links["k"]
            steps = {}

            def stats(l, src, st_, mv_, signal):
                l.done(dve.bn_stats(st_[:], src[:]))
                l.wait_apart()
                l.done(dve.bn_aggr(mv_[:], st_[:]))
                l.wait()
                dve.tensor_scalar_add(mv_[:, 1:2], mv_[:, 1:2], 1e-5).then_inc(s[signal], 1)

            def normed(src, mv_, rs_, out, root, signal, free):
                def step(t):
                    dve.wait_ge(s[root], t + 1)
                    wait_past(dve, s[free], t)
                    dve.tensor_scalar(out[:], src[:], mv_[:, 0:1], rs_[:, 0:1], ALU.subtract, ALU.mult)\
                       .then_inc(s[signal], 1)
                return step

            def stats1(t):
                dve.wait_ge(s["x_in"], 16 * (t + 1))
                stats(lx, x, st, mv, "var1")
            steps["x.stats"] = stats1
            steps["x.norm"] = normed(x, mv, rstd, xn, "root1", "xn_ready", "xnT_ps")

            def take_q(k):
                def step(t):
                    dve.wait_ge(s["q_ps"], 4 * t + k + 1)
                    dve.tensor_copy(q[:, :, 4 * k:4 * k + 4, :].rearrange("c b h q -> c h b q"),
                                    x0[0:CD, :].rearrange("c (h b q) -> c h b q", h=4, b=2)).then_inc(s["qd_sb"], 1)
                return step
            steps["x.q1"], steps["x.q3"] = take_q(1), take_q(3)

            def maxes(k):
                def step(t):
                    dve.wait_ge(s["sc_ps"], 4 * t + k + 1)
                    dve.tensor_reduce(negmax[:, k, :], xbank[1 - k % 2].rearrange("p (i m) -> p i m", i=4),
                                      AX.X, ALU.max, negate=True).then_inc(s["max_done"], 1)
                return step

            def rrows(k):
                def step(t):
                    dve.wait_ge(s["exp_done"], 4 * t + k + 1)
                    dve.reciprocal(rrow[:, k, :], rowsum[:, k, :]).then_inc(s["rrow_done"], 1)
                return step
            for k in range(4):
                steps[f"x.x{k}"], steps[f"x.r{k}"] = maxes(k), rrows(k)

            def add_cross(t):
                dve.wait_ge(s["xo_ps"], t + 1)
                dve.wait_ge(s["xr_in"], 16 * (t + 1))
                wait_past(dve, s["x3_ready"], t)
                dve.tensor_tensor(x2[:], xr[:], x1[:, 0:D], ALU.add).then_inc(s["x2_ready"], 1)
                dve.wait_ge(s["x2_ready"], t + 1)
                stats(ly, x2, st2, mv2, "var2")
            steps["y.add"] = add_cross
            steps["y.norm2"] = normed(x2, mv2, rstd2, xn2, "root2", "xn2_ready", "xn2T_ps")

            def alphas(t):
                dve.wait_ge(s["expz_done"], t + 1)
                lt.done(dve.tensor_scalar_add(alpha[:], alpha[:], 1.0))
                lt.wait()
                lt.done(dve.reciprocal(alpha[:], alpha[:]))
                lt.wait()
                dve.tensor_scalar(alpha[:], alpha[:], 2.0, -1.0, ALU.mult, ALU.add).then_inc(s["alpha_done"], 1)
            steps["t.alpha"] = alphas

            def tree_norm(t):
                dve.wait_ge(s["actx_ps"], t + 1)
                m = t0[0:N, 0:AH * 18].rearrange("q (h b d) -> q h b d", h=AH, b=2)
                lt.done(dve.reciprocal(arz[:], m[:, :, :, AD]))
                lt.wait()
                for b in range(2):
                    ins = dve.tensor_tensor(actx[:, b, :].rearrange("q (h d) -> q h d", h=AH), m[:, :, b, 0:AD],
                                            arz[:, :, b].unsqueeze(2).to_broadcast([N, AH, AD]), ALU.mult)
                ins.then_inc(s["actx_ready"], 1)
            steps["t.norm"] = tree_norm

            def add_tree(t):
                dve.wait_ge(s["ao_ps"], t + 1)
                wait_past(dve, s["x3b_ready"], t)
                dve.tensor_tensor(x3[:], x2[:], t0[:, 0:D], ALU.add).then_inc(s["x3_ready"], 1)
                dve.wait_ge(s["x3_ready"], t + 1)
                stats(lt, x3, st3, mv3, "var3")
            steps["t.add"] = add_tree
            steps["t.norm3"] = normed(x3, mv3, rstd3, xn3, "root3", "xn3_ready", "xn3T_ps")

            t0k = t0.rearrange("p (k i) -> p k i", k=NQ)

            def split(t):
                dve.wait_ge(s["key_ps"], t + 1)
                dve.nop(nofuse=True)
                for k in range(NQ):
                    ins = dve.max(top[:, k, :], t0k[:, k, :])
                lk.done(ins)
                lk.wait()
                lk.done(dve.tensor_tensor(u[:], t0k, top[:, :, 0:1].to_broadcast([128, NQ, NSQ]), ALU.subtract))
                lk.done(dve.tensor_tensor(tops[:, :, 0:8], top[:], top[:, :, 0:1].to_broadcast([128, NQ, 8]),
                                          ALU.subtract))
                lk.wait()
                uh = u[:].rearrange("p (h e) i -> p h (e i)", h=FH)
                lk.done(dve.tensor_scalar_max(us[:, :, 0, :], uh, FLOOR))
                lk.wait()
                dve.scalar_tensor_tensor(out=us[:, :, 1, :], in0=uh, scalar=FLOOR, in1=us[:, :, 0, :],
                                         op0=ALU.max, op1=ALU.subtract).then_inc(s["us_ready"], 1)
            steps["k.split"] = split

            def tops2(t):
                lk.wait_apart()
                for k in range(NQ):
                    ins = dve.match_replace(u2[:, k, :], tops[:, k, 0:8], u[:, k, :], DROPPED)
                lk.done(ins)
                lk.wait_apart()
                for k in range(NQ):
                    ins = dve.max(tops[:, k, 8:16], u2[:, k, :])
                lk.done(ins)
            steps["k.tops"] = tops2

            def candidates(t):
                lk.wait()
                tv = tops[:].rearrange("p (h e) r -> p h e r", e=2)
                at, i = 0, 0
                while i <= TOPK:
                    w = CAND[i]
                    n = CAND.count(w)
                    shape = [128, FH, n, w]
                    dst = cand[:, :, at:at + n * w].rearrange("p h (n w) -> p h n w", n=n)
                    lk.done(dve.tensor_tensor(dst, tv[:, :, 0, i:i + n].unsqueeze(3).to_broadcast(shape),
                                              tv[:, :, 1, 0:w].unsqueeze(2).to_broadcast(shape), ALU.add))
                    at += n * w
                    i += n
                lk.wait_apart()
                for h in range(FH):
                    ins = dve.max(best[:, h, 0:8], cand[:, h, :])
                lk.done(ins)
                lk.wait_apart()
                for h in range(FH):
                    ins = dve.match_replace(cand2[:, h, :], best[:, h, 0:8], cand[:, h, :], DROPPED)
                lk.done(ins)
                lk.wait_apart()
                for h in range(FH):
                    ins = dve.max(best[:, h, 8:16], cand2[:, h, :])
                ins.then_inc(s["best_ready"], 1)
                dve.wait_ge(s["best_ready"], t + 1)
                wait_past(dve, s["usE_ready"], t)
                lk.done(dve.tensor_tensor(cut[:], best[:, :, TOPK - 1], best[:, :, TOPK], ALU.add))
                lk.wait()
                lk.done(dve.tensor_scalar_mul(cut[:], cut[:], 0.5))
            steps["k.cand"] = candidates

            def weight_sum(t):
                dve.wait_ge(s["ebest_done"], t + 1)
                lk.done(dve.reduce_sum(z[:], ebest[:], AX.X))
                lk.wait()
                dve.reciprocal(rz[:], z[:]).then_inc(s["rz_ready"], 1)
            steps["k.z"] = weight_sum

            def carry(t):
                dve.wait_ge(s["usT_sb"], t + 1)
                dve.wait_ge(s["lnz_ready"], t + 1)
                wait_past(dve, s["mw_done"], FH * t)
                wait_past(dve, s["h_ps"], t)
                dve.tensor_copy(xn3T[:], xn3K[:])
                dve.tensor_copy(lnzE[:], lnz[:])
                dve.tensor_copy(cutE[:], cut[:])
                dve.tensor_copy(usT[:], usK[:]).then_inc(s["usE_ready"], 1)
            steps["e.us"] = carry

            def mask(h):
                def step(t):
                    dve.wait_ge(s["ew_done"], FH * t + h + 1)
                    if h < NMW:
                        wait_past(dve, s["wsum_step"], (FH - 1) * t + h - (FH - 1 - NMW))
                    else:
                        dve.wait_ge(s["wsum_step"], (FH - 1) * t + max(h - NMW, 1))
                    dve.scalar_tensor_tensor(out=mw[:, h % NMW, :], in0=sslot[h % 2][:, :], scalar=cutE[:, h:h + 1],
                                             in1=ew[:, h % 2, :], op0=ALU.is_ge, op1=ALU.mult)\
                       .then_inc(s["mw_done"], 1)
                return step
            for h in range(FH):
                steps[f"e.w{h}"] = mask(h)

            def gate(t):
                dve.wait_ge(s["wsum_step"], (FH - 1) * (t + 1))
                wait_past(dve, s["gT_ps"], t)
                dve.tensor_tensor(g[:], wsum[:], gh[:], ALU.mult).then_inc(s["g_ready"], 1)
            steps["e.gate"] = gate

            def add_experts(t):
                dve.wait_ge(s["y_ps"], t + 1)
                wait_past(dve, s["out_done"], 16 * t)
                dve.tensor_tensor(y[:], x3c[:], f0[:, 0:D], ALU.add).then_inc(s["y_ready"], 1)
            steps["e.add"] = add_experts

            def begin(stage, t):
                if stage in links:
                    links[stage].begin(t)
            run(dve, steps, DVE_ORDER, begin)
            assert all(l.n == l.per_tile for l in links.values()), [l.n for l in links.values()]

        @block.gpsimd
        def _(pool):
            pool.memset(halfneg[:], -0.5).then_inc(s["pool_set"], 1)
            pool.memset(feat[:, :, 0:1], 1.0).then_inc(s["pool_set"], 1)
            pool.memset(vblk[:], 0.0).then_inc(s["pool_set"], 1)
            pool.wait_ge(s["pool_set"], 3)
            for b in range(2):
                pool.memset(vblk[N * b:N * b + N, :, b, AD:AD + 1], 1.0).then_inc(s["pool_set"], 1)
            pool.wait_ge(s["pool_set"], 5)
            pool.wait_ge(s["wload"], 16 * len(WEIGHTS))
            steps = {}

            def root(variance, mv_, rs_, signal):
                def step(t):
                    pool.wait_ge(s[variance], t + 1)
                    pool.tensor_tensor(rs_[:], mv_[:, 1:2], halfneg[:], ALU.pow).then_inc(s[signal], 1)
                return step
            steps["x.root"] = root("var1", mv, rstd, "root1")
            steps["y.root2"] = root("var2", mv2, rstd2, "root2")
            steps["t.root3"] = root("var3", mv3, rstd3, "root3")

            def norm(k):
                def step(t):
                    pool.wait_ge(s["rrow_done"], 4 * t + k + 1)
                    pool.tensor_tensor(p[:, k, :, :], p[:, k, :, :],
                                       rrow[:, k, :].unsqueeze(2).to_broadcast([128, 4, M]), ALU.mult)\
                        .then_inc(s["norm_done"], 1)
                return step
            for k in range(4):
                steps[f"x.n{k}"] = norm(k)

            def features(t):
                pool.wait_ge(s["alpha_done"], t + 1)
                for l in range(DEPTH):
                    w = 2 ** l
                    ins = pool.tensor_tensor(feat[:, :, w:2 * w], feat[:, :, 0:w],
                                             alpha[:, :, l:l + 1].to_broadcast([128, AH, w]), ALU.mult)
                    if l < DEPTH - 1:
                        ins.then_inc(s["pool_t"], 1)
                        pool.wait_ge(s["pool_t"], (DEPTH - 1) * t + l + 1)
                ins.then_inc(s["feat_ready"], 1)
            steps["t.feat"] = features

            def causal(t):
                pool.wait_ge(s["sime"], t + 1)
                pool.tensor_tensor(am[:].rearrange("p r c q -> p (r c) q"), ap_[:].rearrange("p r c q -> p (r c) q"),
                                   cmask[:].unsqueeze(1).to_broadcast([128, AH, N]), ALU.mult)\
                    .then_inc(s["am_done"], 1)
            steps["t.mask"] = causal

            def keep(src, dst, filled, reader, signal):
                def step(t):
                    pool.wait_ge(s[filled], t + 1)
                    wait_past(pool, s[reader], t)
                    pool.nop(nofuse=True)
                    pool.tensor_copy(dst[:], src[:]).then_inc(s[signal], 1)
                return step
            steps["k.keep"] = keep(x3, x3b, "x3_ready", "x3c_ready", "x3b_ready")
            steps["e.keep"] = keep(x3b, x3c, "x3b_ready", "y_ready", "x3c_ready")

            def add_weights(h):
                def step(t):
                    pool.wait_ge(s["mw_done"], FH * t + h + 1)
                    if h == 1:
                        wait_past(pool, s["g_ready"], t)
                    else:
                        pool.wait_ge(s["wsum_step"], (FH - 1) * t + h - 1)
                    pool.tensor_tensor(wsum[:], mw[:, 0, :] if h == 1 else wsum[:], mw[:, h % NMW, :],
                                       ALU.add).then_inc(s["wsum_step"], 1)
                return step
            for h in range(1, FH):
                steps[f"e.a{h}"] = add_weights(h)
            run(pool, steps, POOL_ORDER)


PE_ORDER = """
    k.turn3 e.s0 e.hid k.key y.m0 y.m1 e.s1 e.s2 y.m2 k.kturn y.m3 e.s3 y.out x.turn e.s4 x.q0 e.s5 x.q1
    t.turn x.q2 t.pv e.s6 x.q3 e.s7 x.s0 t.feat x.s1 t.sim x.s2 x.s3 t.mix e.gturn x.p0 t.cturn x.p1
    t.out e.out x.p2 x.p3
""".split()
ACT_ORDER = """
    e.e0 k.turn3 e.gelu y.m0 e.e1 y.m1 y.m2 y.m3 e.e2 e.e3 k.kturn x.turn e.e4 x.q0 e.e5 t.turn t.alpha
    x.q2 e.e6 t.v e.e7 t.feat x.e0 t.exp x.e1 x.e2 k.ebest x.e3 e.gturn t.cturn x.p0 x.p1 k.lnz x.p2
    x.p3
""".split()
DVE_ORDER = """
    e.us x.stats x.norm e.w0 k.split e.w1 k.tops e.w2 y.add e.w3 e.w4 y.norm2 x.q1 e.w5 t.alpha x.q3
    e.w6 x.x0 e.w7 x.x1 k.cand x.x2 x.r0 e.gate x.x3 x.r1 x.r2 k.z t.norm x.r3 t.add t.norm3 e.add
""".split()
POOL_ORDER = """
    x.root e.keep k.keep e.a1 e.a2 y.root2 e.a3 e.a4 t.feat e.a5 e.a6 e.a7 t.mask x.n0 x.n1 x.n2 x.n3
    t.root3
""".split()



def kernel(**inputs):
    import concourse.bacc as bacc
    from concourse.bass_utils import run_bass_kernel_spmd

    w = {k: np.asarray(v) for k, v in inputs.items()}
    cc = np.ascontiguousarray
    keys = np.zeros((128, 4, 2 * NSQ), np.float32)
    for i in range(4):
        keys[32 * i:32 * i + DQH, i, 0:NSQ] = w["L0_ffn_K1"].T
        keys[32 * i + DQH:32 * i + 2 * DQH, i, NSQ:] = w["L0_ffn_K2"].T
    pair = np.arange(NE)
    one = np.concatenate([np.arange(NSQ)[:, None] == pair // NSQ, np.arange(NSQ)[:, None] == pair % NSQ])
    last = np.array([0] + [f.bit_length() for f in range(1, NF)])
    weight = np.array([sum(2.0 ** -d for d in range(max(l, 1), DEPTH + 1)) for l in last]) / DEPTH
    arrays = {
        "x": cc(w["x"].reshape(B * N, D)), "c": cc(w["ctx_768"]), "cT": cc(w["ctx_768"].transpose(0, 2, 1)),
        "ident": np.eye(128, dtype=np.float32), "ident16": np.eye(128, dtype=np.float16),
        "sel": np.concatenate([one, one]).astype(np.float16),
        "cmask": (np.arange(N)[None, :] >= (np.arange(128) % N)[:, None]).astype(np.float32),
        "rootc": np.tile(np.sqrt(weight), 2).astype(np.float32)[:, None],
        "wqT": cc(w["L0_xattn_Wq"].T), "wkT": cc(w["L0_xattn_Wk"].T), "wvT": cc(w["L0_xattn_Wv"].T),
        "wo": cc(w["L0_xattn_Wo"]), "bo": w["L0_xattn_bo"][None, :],
        "wp": w["L0_attn_Wp"], "bp": w["L0_attn_bp"][None, :], "awv": w["L0_attn_Wv"], "awo": w["L0_attn_Wo"],
        "fwqT": cc(w["L0_ffn_Wq"].T), "fbqT": cc(w["L0_ffn_bq"].reshape(2, 128).T), "keys": keys,
        "wdT": cc(w["L0_ffn_W_down"][0:NE].T), "wup": cc(w["L0_ffn_W_up"][0:NE]),
    }
    nc = bacc.Bacc("TRN2", target_bir_lowering=False, num_devices=1)
    aps = {k: nc.dram_tensor(k + "_dram", v.shape, mybir.dt.from_np(v.dtype), kind="ExternalInput").ap()
           for k, v in arrays.items()}
    aps["y"] = nc.dram_tensor("y_dram", (B * N, D), mybir.dt.float32, kind="ExternalOutput").ap()
    build(nc, aps)
    r = run_bass_kernel_spmd(nc, [{k + "_dram": v for k, v in arrays.items()}], core_ids=[0])
    return r.results[0]["y_dram"].reshape(B, N, D)
```

```python
from contextlib import ExitStack

import numpy as np
import concourse.bass as bass
from concourse import mybir

B, N, D = 64, 64, 128
M, CD = 128, 96
XH, XD = 16, 64
AH, DEPTH, AD = 16, 5, 8
NF = 2 ** DEPTH
FH, NSQ, TOPK, DQH = 8, 32, 10, 16
NE = NSQ * NSQ
PAIR = 2 * N
NT = B * N // PAIR
XHP, AHP = XH // 2, AH // 2
EC = NE // 128
NQ = 2 * FH
DROPPED = -3.0e38
NMW = 4
QSCALE = 256.0
FLOOR = -30000.0

CAND = [(TOPK + 1) // (i + 1) for i in range(TOPK + 1)]
NCAND = sum(CAND)


def build(nc, a):
    f32, f16 = mybir.dt.float32, mybir.dt.float16
    ALU, ACT, AX = mybir.AluOpType, mybir.ActivationFunctionType, mybir.AxisListType
    ctx = ExitStack()
    with ctx:
        def sb(name, shape, dt=f32):
            return ctx.enter_context(nc.sbuf_tensor(name, shape, dt))

        def sem(name):
            return ctx.enter_context(nc.semaphore(name))

        ident = sb("ident", [128, 128])
        ident16 = sb("ident16", [128, 128], f16)
        sel = sb("sel", [128, NE], f16)
        cneg = sb("cneg", [128, AHP * N], f16)
        rootc = sb("rootc", [2 * NF, 1])
        ones16 = sb("ones16", [96, 128], f16)
        bias = sb("bias", [96, FH * 2 * NSQ + D + AH * DEPTH])
        bias16 = sb("bias16", [96, FH * 2 * NSQ + D + AH * DEPTH], f16)
        halfneg = sb("halfneg", [128, 1])
        wqT = sb("wqT", [128, XHP, D])
        wkT = sb("wkT", [128, XHP, CD])
        wvT = sb("wvT", [128, XHP, CD])
        wo = sb("wo", [128, XHP, D])
        wp = sb("wp", [D, AH * DEPTH])
        awv = sb("awv", [D, D])
        awo = sb("awo", [D, D])
        fwqT = sb("fwqT", [128, 2, D])
        fbqT = sb("fbqT", [128, 2, 96])
        keys = sb("keys", [128, 4, 2 * NSQ])
        wdT = sb("wdT", [D, NE])
        wup = sb("wup", [128, EC, D])
        qk = sb("qk", [D, XH, CD])
        vo = sb("vo", [CD, XH, D])
        fqk = sb("fqk", [D, FH * 2 * NSQ])
        qk16 = sb("qk16", [D, 2, XH, CD], f16)
        fqk16 = sb("fqk16", [D, 2, FH * 2 * NSQ], f16)
        wd16 = sb("wd16", [D, 2, NE], f16)
        x = sb("x", [128, D])
        c0 = sb("c0", [M, 2, CD])
        cT = sb("cT", [CD, 2, M])
        st = sb("st", [128, 6])
        mv = sb("mv", [128, 2])
        rstd = sb("rstd", [128, 1])
        xn = sb("xn", [128, D])
        xnT = sb("xnT", [D, 2, 128], f16)
        q = sb("q", [CD, 2, XH, N])
        negmax = sb("negmax", [128, 4, 4])
        rowsum = sb("rowsum", [128, 4, 4])
        rrow = sb("rrow", [128, 4, 4])
        p = sb("p", [128, 4, 4, M])
        pT = sb("pT", [M, 4, 8 * N])
        uT = sb("uT", [CD, XH, 2, N])
        x2 = sb("x2", [128, D])
        st2 = sb("st2", [128, 6])
        mv2 = sb("mv2", [128, 2])
        rstd2 = sb("rstd2", [128, 1])
        xn2 = sb("xn2", [128, D])
        xn2T = sb("xn2T", [D, 128])
        alpha = sb("alpha", [128, AH, DEPTH])
        feat = sb("feat", [128, AH, NF])
        featT = sb("featT", [2 * NF, AHP, 128])
        vblk = sb("vblk", [128, AH, 2, AD + 1])
        am = sb("am", [128, 2, AHP, N])
        arz = sb("arz", [N, AH, 2])
        actx = sb("actx", [N, 2, AH * AD])
        actxT = sb("actxT", [D, 128])
        x3 = sb("x3", [128, D])
        st3 = sb("st3", [128, 6])
        mv3 = sb("mv3", [128, 2])
        rstd3 = sb("rstd3", [128, 1])
        xn3 = sb("xn3", [128, D])
        xn3T = sb("xn3T", [D, 2, 128], f16)
        top = sb("top", [128, NQ, 8])
        tops = sb("tops", [128, NQ, 16])
        u = sb("u", [128, NQ, NSQ])
        u2 = sb("u2", [128, NQ, NSQ])
        lnz = sb("lnz", [128, FH])
        x3b = sb("x3b", [128, D])
        xn3K = sb("xn3K", [D, 2, 128], f16)
        usK = sb("usK", [128, FH, 128], f16)
        lnzE = sb("lnzE", [128, FH])
        cutE = sb("cutE", [128, FH])
        x3c = sb("x3c", [128, D])
        xr = sb("xr", [128, D])
        us = sb("us", [128, FH, 2, 2 * NSQ], f16)
        usT = sb("usT", [128, FH, 128], f16)
        cand = sb("cand", [128, FH, NCAND])
        cand2 = sb("cand2", [128, FH, NCAND])
        best = sb("best", [128, FH, 16])
        cut = sb("cut", [128, FH])
        ebest = sb("ebest", [128, FH, TOPK])
        z = sb("z", [128, FH])
        rz = sb("rz", [128, FH])
        gh = sb("gh", [128, NE])
        ew = sb("ew", [128, 2, NE])
        mw = sb("mw", [128, NMW, NE])
        wsum = sb("wsum", [128, NE])
        g = sb("g", [128, NE])
        gT = sb("gT", [128, EC, 128])
        y = sb("y", [128, D])

        psX = ctx.enter_context(nc.psum_tensor("psX", [128, 2, 512], f32))
        psT = ctx.enter_context(nc.psum_tensor("psT", [128, 2, 512], f32))
        psF = ctx.enter_context(nc.psum_tensor("psF", [128, 4, 512], f32))
        x0, x1 = psX[:, 0, :], psX[:, 1, :]
        t0, t1 = psT[:, 0, :], psT[:, 1, :]
        t01 = psT[:].rearrange("p a b -> p (a b)")
        t0h = t0.bitcast(f16)
        f0 = psF[:, 0:2, :].rearrange("p a b -> p (a b)")
        f1 = psF[:, 2:4, :].rearrange("p a b -> p (a b)")
        xbank = [x0, x1]
        sslot = [f1, f0, f1, f0, f0, f1, f0, f1]

        names = """wqk_load wload ones_set setup_ps setup_sb high_set split_done x_in xr_in c_in cT_in out_done
            dve_x dve_y dve_t dve_k pool_set pool_t
            var1 root1 xn_ready xnT_ps xnT_sb xnL_sb q_ps q1_taken q0_taken
            sc_ps max_done exp_done rrow_done norm_done pT_ps pT_sb u_ps u_sb xo_ps x2_ready
            var2 root2 xn2_ready xn2T_ps xn2T_sb pv_ps alpha_done v_sb feat_ready featT_ps featT_sb
            sim_ps am_ready actx_ps actx_ready actxT_ps actxT_sb ao_ps x3_ready var3 root3 xn3_ready
            xn3T_ps xn3T_sb xn3L_sb key_ps us_ready usT_ps usT_sb best_ready ebest_done rz_ready lnz_ready usE_ready
            x3b_ready x3c_ready h_ps gelu_done s_ps ew_done mw_done wsum_step g_ready gT_ps gT_sb y_ps y_ready""".split()
        s = {n: sem(n) for n in names}
        block = ctx.enter_context(nc.Block())

        WEIGHTS = [(wqT, a["wqT"].rearrange("(c p) d -> p c d", p=128)),
                   (wkT, a["wkT"].rearrange("(c p) d -> p c d", p=128)),
                   (wvT, a["wvT"].rearrange("(c p) d -> p c d", p=128)),
                   (wo, a["wo"].rearrange("(c p) d -> p c d", p=128)),
                   (fwqT, a["fwqT"].rearrange("(c p) d -> p c d", p=128)),
                   (fbqT, a["fbqT"]), (keys, a["keys"]),
                   (ident, a["ident"]), (bias[:, 512:640], a["bo"]), (wp, a["wp"]), (bias[:, 640:720], a["bp"]), (awv, a["awv"]),
                   (awo, a["awo"]), (rootc, a["rootc"]), (cneg, a["cneg"]),
                   (ident16, a["ident16"]), (sel, a["sel"]), (wdT, a["wdT"]),
                   (wup, a["wup"].rearrange("(c p) d -> p c d", p=128))]
        xt = a["x"].rearrange("(t p) d -> t p d", p=128)
        ct = a["c"].rearrange("(t b) m c -> t m b c", b=2)
        ctT = a["cT"].rearrange("(t b) c m -> t c b m", b=2)
        yt = a["y"].rearrange("(t p) d -> t p d", p=128)

        def run(eng, steps, order, begin=None, begin_turn=None):
            assert sorted(order) == sorted(steps), set(order) ^ set(steps)
            lag = {"x": 0, "y": 1, "t": 1, "k": 2, "e": 3}

            def turn(t, stages):
                if begin_turn:
                    begin_turn(stages)
                if begin:
                    for st in stages:
                        begin(st, t - lag[st])
                for name in order:
                    if name[0] in stages:
                        steps[name](t - lag[name[0]])

            turn(0, "x")
            turn(1, "xyt")
            turn(2, "xytk")
            turn(3, "xytke")
            with eng.Fori(4, NT, 2) as t:
                turn(t, "xytke")
                turn(t + 1, "xytke")
            turn(NT, "ytke")
            turn(NT + 1, "ke")
            turn(NT + 2, "e")

        def wait_past(eng, sm, count):
            if not (isinstance(count, int) and count <= 0):
                eng.wait_ge(sm, count)

        @block.sync
        def _(sp):
            def after(name, count):
                sp.wait_ge(s[name], count)
                sp.nop(nofuse=True)

            def load_scores(t):
                if not isinstance(t, int) or t > 0:
                    after("xn_ready", t)
                sp.dma_start(x[:], xt[t]).then_inc(s["x_in"], 16)
                if not isinstance(t, int) or t > 0:
                    after("sc_ps", 4 * t)
                sp.dma_start(cT[:], ctT[t]).then_inc(s["cT_in"], 16)

            def load_mix(t):
                if not isinstance(t, int) or t > 0:
                    after("u_ps", 4 * t)
                sp.dma_start(c0[:], ct[t]).then_inc(s["c_in"], 16)
                if not isinstance(t, int) or t > 0:
                    after("x2_ready", t)
                sp.dma_start(xr[:], xt[t]).then_inc(s["xr_in"], 16)

            def store(t):
                after("y_ready", t + 1)
                sp.dma_start(yt[t], y[:]).then_inc(s["out_done"], 16)

            for i, (dst, src) in enumerate(WEIGHTS):
                sp.dma_start(dst if isinstance(dst, bass.AP) else dst[:], src)\
                    .then_inc(s["wqk_load" if i < 2 else "wload"], 16)
            load_scores(0)
            for t in range(1, 4):
                load_scores(t)
                load_mix(t - 1)
            with sp.Fori(4, NT) as t:
                load_scores(t)
                load_mix(t - 1)
                store(t - 4)
            load_mix(NT - 1)
            for t in range(NT - 4, NT):
                store(t)
            sp.wait_ge(s["out_done"], 16 * NT)

        @block.tensor
        def _(pe):
            pe.wait_ge(s["wqk_load"], 16 * 2)
            pe.wait_ge(s["ones_set"], 4)

            def setup_round(n, mms):
                if n >= 2:
                    pe.wait_ge(s["setup_sb"], n - 1)
                if n == 4:
                    pe.wait_ge(s["wload"], 16 * (len(WEIGHTS) - 2))
                for out, lhsT, rhs in mms:
                    mm = pe.matmul(out, lhsT, rhs, start=True, stop=True)
                mm.then_inc(s["setup_ps"], 1)

            for n, (lw, rw, w, rows) in enumerate(((wqT, wkT, CD, D), (wvT, wo, D, CD))):
                for j in range(4):
                    mms = []
                    for i in range(4):
                        h = 4 * j + i
                        r = XD * (h % 2)
                        mms.append((psF[0:rows, h % 2 + 2 * (j % 2), (i // 2) * w:(i // 2 + 1) * w],
                                    lw[r:r + XD, h // 2, :], rw[r:r + XD, h // 2, :]))
                    setup_round(4 * n + j, mms)
            kflat = keys[:].rearrange("p g i -> p (g i)")
            setup_round(8, [(x0[:, 256 * c:256 * c + 256], fwqT[:, c, :], kflat) for c in range(2)])
            setup_round(9, [(x1[0:96, 256 * c:256 * c + 256], fbqT[:, c, :], kflat) for c in range(2)])
            pe.wait_ge(s["setup_sb"], 10)

            pe.wait_ge(s["split_done"], 4)

            def product(out, left, right, open_group=False):
                pe.matmul(out, left[:, 0, :], right[:, 0, :], start=not open_group, stop=False)
                pe.matmul(out, left[:, 0, :], right[:, 1, :], start=False, stop=False)
                return pe.matmul(out, left[:, 1, :], right[:, 0, :], start=False, stop=True)

            steps = {}

            def x_turn(t):
                pe.wait_ge(s["xn_ready"], t + 1)
                wait_past(pe, s["u_sb"], 4 * t)
                pe.transpose(x0[:, 0:128], xn[:], ident[:]).then_inc(s["xnT_ps"], 1)
            steps["x.turn"] = x_turn

            def queries(k):
                def step(t):
                    if k == 0:
                        pe.wait_ge(s["xnT_sb"], t + 1)
                        pe.wait_ge(s["xnL_sb"], t + 1)
                        wait_past(pe, s["x2_ready"], t)
                    elif k == 2:
                        pe.wait_ge(s["q1_taken"], 2 * t + 1)
                    elif k == 3:
                        pe.wait_ge(s["q0_taken"], 2 * t + 1)
                    for i in range(4):
                        mm = product(xbank[1 - k % 2][0:CD, i * 128:i * 128 + 128], qk16[:, :, 4 * k + i, :], xnT)
                    mm.then_inc(s["q_ps"], 1)
                return step

            def scores(k):
                def step(t):
                    pe.wait_ge(s["cT_in"], 16 * (t + 1))
                    if k < 2:
                        pe.wait_ge(s["q1_taken"], 2 * t + 2)
                        pe.wait_ge(s["q0_taken"], 2 * t + 2)
                    else:
                        pe.wait_ge(s["exp_done"], 4 * t + k - 1)
                    b = k // 2
                    for i in range(4):
                        h = 8 * (k % 2) + 2 * i
                        mm = pe.matmul(xbank[1 - k % 2][:, i * M:i * M + M],
                                       q[:, b, h:h + 2, :].rearrange("c h q -> c (h q)"),
                                       cT[:, b, :], start=True, stop=True)
                    mm.then_inc(s["sc_ps"], 1)
                return step

            def probs_turn(k):
                def step(t):
                    if k < 2:
                        pe.wait_ge(s["exp_done"], 4 * t + k + 3)
                    else:
                        pe.wait_ge(s["pT_sb"], 4 * t + k - 1)
                    pe.wait_ge(s["norm_done"], 4 * t + k + 1)
                    for i in range(4):
                        mm = pe.transpose(xbank[1 - k % 2][:, i * 128:i * 128 + 128], p[:, k, i, :], ident[:])
                    mm.then_inc(s["pT_ps"], 1)
                return step

            def mix(k):
                def step(t):
                    pe.wait_ge(s["c_in"], 16 * (t + 1))
                    if k < 2:
                        pe.wait_ge(s["pT_sb"], 4 * t + k + 3)
                    else:
                        pe.wait_ge(s["u_sb"], 4 * t + k - 1)
                    pe.matmul(xbank[1 - k % 2][0:CD, :], c0[:, k // 2, :], pT[:, k, :],
                              start=True, stop=True).then_inc(s["u_ps"], 1)
                return step

            for k in range(4):
                steps[f"x.q{k}"], steps[f"x.s{k}"] = queries(k), scores(k)
                steps[f"x.p{k}"], steps[f"y.m{k}"] = probs_turn(k), mix(k)

            def cross_out(t):
                pe.wait_ge(s["u_sb"], 4 * t + 4)
                pe.matmul(x1[:, 0:D], ones16[:], bias16[:, 512:640], start=True, stop=False)
                for h in range(XH):
                    mm = pe.matmul(x1[:, 0:D], uT[:, h, :, :].rearrange("c b q -> c (b q)"), vo[:, h, :],
                                   start=False, stop=(h == XH - 1))
                mm.then_inc(s["xo_ps"], 1)
            steps["y.out"] = cross_out

            def t_turn(t):
                pe.wait_ge(s["xn2_ready"], t + 1)
                wait_past(pe, s["xn3L_sb"], t)
                pe.transpose(t1[:, 0:128], xn2[:], ident[:]).then_inc(s["xn2T_ps"], 1)
            steps["t.turn"] = t_turn

            def paths_values(t):
                pe.wait_ge(s["xn2T_sb"], t + 1)
                pe.matmul(t1[:, 0:AH * DEPTH], ones16[:], bias16[:, 640:720], start=True, stop=False)
                pe.matmul(t1[:, 0:AH * DEPTH], xn2T[:], wp[:], start=False, stop=True)
                pe.matmul(t1[:, 128:256], xn2T[:], awv[:], start=True, stop=True).then_inc(s["pv_ps"], 1)
            steps["t.pv"] = paths_values

            def feat_turn(t):
                pe.wait_ge(s["feat_ready"], t + 1)
                wait_past(pe, s["usT_sb"], t)
                pe.wait_ge(s["v_sb"], 2 * t + 2)
                pe.nop(nofuse=True)
                ff = feat[:].rearrange("p (c r) f -> p c (r f)", c=AHP)
                for c in range(AHP):
                    mm = pe.transpose(t01[0:2 * NF, c * 128:c * 128 + 128], ff[:, c, :], ident[:])
                mm.then_inc(s["featT_ps"], 1)
            steps["t.feat"] = feat_turn

            def similarity(t):
                pe.wait_ge(s["featT_sb"], t + 1)
                for r in range(2):
                    pe.matmul(psT[:, r, :], ident16[:], cneg[:], start=True, stop=False)
                for c in range(AHP):
                    for b in range(2):
                        for r in range(2):
                            ft = featT[NF * r:NF * r + NF, c, N * b:N * b + N]
                            mm = pe.matmul(psT[N * b:N * b + N, r, c * N:c * N + N], ft, ft,
                                           start=False, stop=(c == AHP - 1), tile_position=(NF * r, N * b))
                mm.then_inc(s["sim_ps"], 1)
            steps["t.sim"] = similarity

            def tree_mix(t):
                pe.wait_ge(s["am_ready"], t + 1)
                for h in range(AH):
                    mm = pe.matmul(t0[0:N, h * 18:h * 18 + 18], am[:, h % 2, h // 2, :],
                                   vblk[:, h, :, :].rearrange("p b d -> p (b d)"), start=True, stop=True)
                mm.then_inc(s["actx_ps"], 1)
            steps["t.mix"] = tree_mix

            def tree_turn(t):
                pe.wait_ge(s["actx_ready"], t + 1)
                pe.nop(nofuse=True)
                for b in range(2):
                    mm = pe.transpose(t1[:, b * N:b * N + N], actx[:, b, :], ident[0:N, 0:N])
                mm.then_inc(s["actxT_ps"], 1)
            steps["t.cturn"] = tree_turn

            def tree_out(t):
                pe.wait_ge(s["actxT_sb"], t + 1)
                pe.matmul(t0[:, 0:D], actxT[:], awo[:], start=True, stop=True).then_inc(s["ao_ps"], 1)
            steps["t.out"] = tree_out

            def xn3_turn(t):
                pe.wait_ge(s["xn3_ready"], t + 1)
                pe.transpose(t1[:, 0:128], xn3[:], ident[:]).then_inc(s["xn3T_ps"], 1)
            steps["k.turn3"] = xn3_turn

            def key_scores(t):
                pe.wait_ge(s["xn3T_sb"], t + 1)
                pe.wait_ge(s["xn3L_sb"], t + 1)
                pe.matmul(t0, ones16[:], bias16[:, 0:512], start=True, stop=False)
                product(t0, xn3K, fqk16, open_group=True).then_inc(s["key_ps"], 1)
            steps["k.key"] = key_scores

            def keys_turn(t):
                pe.wait_ge(s["us_ready"], t + 1)
                for h in range(FH):
                    mm = pe.transpose(t0h[:, h * 128:h * 128 + 128], us[:, h, :, :].rearrange("p a b -> p (a b)"),
                                      ident16[:])
                mm.then_inc(s["usT_ps"], 1)
            steps["k.kturn"] = keys_turn

            def hidden(t):
                pe.wait_ge(s["usE_ready"], t + 1)
                pe.wait_ge(s["mw_done"], FH * t + 3)
                for j in range(2):
                    cols = slice(j * 512, j * 512 + 512)
                    mm = product(f1[:, cols], xn3T, wd16[:, :, cols])
                mm.then_inc(s["h_ps"], 1)
            steps["e.hid"] = hidden

            def sums(h):
                def step(t):
                    if h == 0:
                        pe.wait_ge(s["usE_ready"], t + 1)
                        wait_past(pe, s["mw_done"], FH * t)
                    elif h == 1:
                        wait_past(pe, s["y_ready"], t)
                    elif h == 5:
                        pe.wait_ge(s["gelu_done"], t + 1)
                    else:
                        pe.wait_ge(s["mw_done"], FH * t + h - (1 if h < 4 else 0 if h == 4 else 1))
                    for j in range(2):
                        mm = pe.matmul(sslot[h][:, j * 512:j * 512 + 512], usT[:, h, :],
                                       sel[:, j * 512:j * 512 + 512], start=True, stop=True)
                    mm.then_inc(s["s_ps"], 1)
                return step
            for h in range(FH):
                steps[f"e.s{h}"] = sums(h)

            def g_turn(t):
                pe.wait_ge(s["g_ready"], t + 1)
                for c in range(EC):
                    mm = pe.transpose(f0[:, c * 128:c * 128 + 128], g[:, c * 128:c * 128 + 128], ident[:])
                mm.then_inc(s["gT_ps"], 1)
            steps["e.gturn"] = g_turn

            def experts_out(t):
                pe.wait_ge(s["gT_sb"], t + 1)
                for c in range(EC):
                    mm = pe.matmul(f0[:, 0:D], gT[:, c, :], wup[:, c, :], start=(c == 0), stop=(c == EC - 1))
                mm.then_inc(s["y_ps"], 1)
            steps["e.out"] = experts_out
            run(pe, steps, PE_ORDER)

        @block.scalar
        def _(act):
            for n, (dst, w, rows, scale) in enumerate(((qk, CD, D, QSCALE * float(XD) ** -0.5), (vo, D, CD, 1.0))):
                for j in range(4):
                    act.wait_ge(s["setup_ps"], 4 * n + j + 1)
                    act.activation(dst[:, 4 * j:4 * j + 4, :].rearrange("p (i e) c -> p e i c", e=2),
                                   psF[0:rows, 2 * (j % 2):2 * (j % 2) + 2, 0:2 * w]
                                   .rearrange("p e (i c) -> p e i c", i=2),
                                   ACT.Copy, scale=scale).then_inc(s["setup_sb"], 1)
            act.wait_ge(s["setup_ps"], 9)
            act.activation(fqk[:], x0, ACT.Copy).then_inc(s["setup_sb"], 1)
            act.wait_ge(s["setup_ps"], 10)
            act.activation(bias[:, 0:512], x1[0:96, :], ACT.Copy).then_inc(s["setup_sb"], 1)

            steps = {}

            def take(name, out, in_, filled, per, k, signal, scale=None, readers=None):
                def step(t):
                    act.wait_ge(s[filled], t * per + k)
                    if readers:
                        wait_past(act, s[readers[0]], readers[1] * t)
                    if scale is None:
                        act.activation(out, in_, ACT.Copy).then_inc(s[signal], 1)
                    else:
                        act.activation(out, in_, ACT.Copy if isinstance(scale, float) else ACT.Identity, scale=scale,
                                       bias=0.0).then_inc(s[signal], 1)
                steps[name] = step

            take("x.turn", xnT[:, 0, :], x0[:, 0:128], "xnT_ps", 1, 1, "xnT_sb")
            for k in (0, 1, 2):
                take(f"x.q{k}", q[:, :, 4 * k:4 * k + 4, :].rearrange("c b h q -> c h b q"),
                     xbank[1 - k % 2][0:CD, :].rearrange("c (h b q) -> c h b q", h=4, b=2), "q_ps", 4, k + 1,
                     "q0_taken" if k % 2 else "q1_taken", scale=1.0 / QSCALE)

            def exps(k):
                def step(t):
                    act.wait_ge(s["max_done"], 4 * t + k + 1)
                    for i in range(4):
                        ins = act.activation(p[:, k, i, :], xbank[1 - k % 2][:, i * M:i * M + M], ACT.Exp,
                                             bias=negmax[:, k, i:i + 1], accum_out=rowsum[:, k, i:i + 1])
                    ins.then_inc(s["exp_done"], 1)
                return step
            for k in range(4):
                steps[f"x.e{k}"] = exps(k)
                take(f"x.p{k}", pT[:, k, :], xbank[1 - k % 2], "pT_ps", 4, k + 1, "pT_sb")
                take(f"y.m{k}", uT[:, 8 * (k % 2):8 * (k % 2) + 8, k // 2, :],
                     xbank[1 - k % 2][0:CD, :].rearrange("c (h q) -> c h q", h=8), "u_ps", 4, k + 1, "u_sb")

            take("t.turn", xn2T[:], t1[:, 0:128], "xn2T_ps", 1, 1, "xn2T_sb")

            stages_now = set()

            def alphas(t):
                act.wait_ge(s["pv_ps"], t + 1)
                wait_past(act, s["feat_ready"], t)
                act.nop(nofuse=True)
                act.preload_act_table_set("gelu_and_others")
                act.activation(alpha[:].rearrange("p h d -> p (h d)"), t1[:, 0:AH * DEPTH], ACT.Tanh,
                               scale=0.5).then_inc(s["alpha_done"], 1)
                if "e" not in stages_now:
                    act.preload_act_table_set("natural_log_exp_and_others")
            steps["t.alpha"] = alphas

            def values(t):
                act.wait_ge(s["pv_ps"], t + 1)
                for b in range(2):
                    act.activation(vblk[N * b:N * b + N, :, b, 0:AD],
                                   t1[N * b:N * b + N, 128:256].rearrange("p (h d) -> p h d", h=AH),
                                   ACT.Copy).then_inc(s["v_sb"], 1)
            steps["t.v"] = values
            take("t.feat", featT[:].rearrange("p c t -> p (c t)"), t01[0:2 * NF, :], "featT_ps", 1, 1, "featT_sb",
                 scale=rootc[:, 0:1])

            def tree_exp(t):
                act.wait_ge(s["sim_ps"], t + 1)
                act.activation(am[:].rearrange("p r c q -> p (r c q)"), t01, ACT.Exp).then_inc(s["am_ready"], 1)
            steps["t.exp"] = tree_exp
            take("t.cturn", actxT[:], t1[:, 0:128], "actxT_ps", 1, 1, "actxT_sb")
            take("k.turn3", xn3K[:, 0, :], t1[:, 0:128], "xn3T_ps", 1, 1, "xn3T_sb", readers=("usE_ready", 1))
            take("k.kturn", usK[:].rearrange("p h t -> p (h t)"), t0h, "usT_ps", 1, 1, "usT_sb",
                 readers=("usE_ready", 1))

            def exp_best(t):
                act.wait_ge(s["best_ready"], t + 1)
                act.activation(ebest[:], best[:, :, 0:TOPK], ACT.Exp).then_inc(s["ebest_done"], 1)
            steps["k.ebest"] = exp_best

            def ln_z(t):
                act.wait_ge(s["rz_ready"], t + 1)
                wait_past(act, s["usE_ready"], t)
                act.activation(lnz[:], rz[:], ACT.Ln).then_inc(s["lnz_ready"], 1)
            steps["k.lnz"] = ln_z

            def gelu(t):
                act.wait_ge(s["h_ps"], t + 1)
                wait_past(act, s["g_ready"], t)
                if "t" not in stages_now:
                    act.nop(nofuse=True)
                    act.preload_act_table_set("gelu_and_others")
                act.activation(gh[:], f1[:, :], ACT.Gelu).then_inc(s["gelu_done"], 1)
                act.preload_act_table_set("natural_log_exp_and_others")
            steps["e.gelu"] = gelu

            def exp_sums(h):
                def step(t):
                    act.wait_ge(s["s_ps"], FH * t + h + 1)
                    if h == 0:
                        act.wait_ge(s["usE_ready"], t + 1)
                    wait_past(act, s["mw_done"], FH * t + max(h - 1, 0))
                    act.activation(ew[:, h % 2, :], sslot[h][:, :], ACT.Exp, bias=lnzE[:, h:h + 1])\
                       .then_inc(s["ew_done"], 1)
                return step
            for h in range(FH):
                steps[f"e.e{h}"] = exp_sums(h)
            take("e.gturn", gT[:].rearrange("p c t -> p (c t)"), f0, "gT_ps", 1, 1, "gT_sb")
            run(act, steps, ACT_ORDER, begin_turn=lambda stages: (stages_now.clear(), stages_now.update(stages)))

        @block.vector
        def _(dve):
            dve.memset(ones16[:], 0.0).then_inc(s["ones_set"], 1)
            dve.wait_ge(s["ones_set"], 1)
            for r in range(3):
                dve.memset(ones16[32 * r:32 * r + 1, :], 1.0).then_inc(s["ones_set"], 1)
            dve.wait_ge(s["wload"], 16 * (len(WEIGHTS) - 2))
            for n, (src, dst) in enumerate(((wdT, wd16), (qk, qk16), (fqk, fqk16))):
                if n >= 1:
                    dve.wait_ge(s["setup_sb"], 4 if n == 1 else 9)
                dve.tensor_copy(dst[:, 0], src[:]).then_inc(s["high_set"], 1)
                dve.wait_ge(s["high_set"], n + 1)
                dve.tensor_tensor(dst[:, 1], src[:], dst[:, 0], ALU.subtract).then_inc(s["split_done"], 1)
            dve.wait_ge(s["setup_sb"], 10)
            dve.tensor_copy(bias16[:], bias[:]).then_inc(s["high_set"], 1)
            dve.wait_ge(s["high_set"], 4)
            dve.tensor_tensor(bias[32:64], bias[32:64], bias16[32:64], ALU.subtract).then_inc(s["high_set"], 1)
            dve.tensor_tensor(bias[64:96], bias[64:96], bias16[64:96], ALU.subtract).then_inc(s["high_set"], 1)
            dve.wait_ge(s["high_set"], 6)
            dve.tensor_copy(bias16[32:64], bias[32:64]).then_inc(s["high_set"], 1)
            dve.tensor_copy(bias16[64:96], bias[64:96]).then_inc(s["high_set"], 1)
            dve.wait_ge(s["high_set"], 8)
            dve.tensor_tensor(bias[64:96], bias[64:96], bias16[64:96], ALU.subtract).then_inc(s["high_set"], 1)
            dve.wait_ge(s["high_set"], 9)
            dve.tensor_copy(bias16[64:96], bias[64:96]).then_inc(s["split_done"], 1)

            class Links:
                def __init__(self, sm, per_tile):
                    self.sm, self.per_tile = sm, per_tile

                def begin(self, t):
                    self.base, self.n = t * self.per_tile, 0

                def done(self, ins):
                    ins.then_inc(self.sm, 1)
                    self.n += 1

                def wait(self):
                    dve.wait_ge(self.sm, self.base + self.n)

                def wait_apart(self):
                    self.wait()
                    dve.nop(nofuse=True)

            links = {"x": Links(s["dve_x"], 2), "y": Links(s["dve_y"], 2), "t": Links(s["dve_t"], 3), "k": Links(s["dve_k"], 16)}
            lx, ly, lt, lk = links["x"], links["y"], links["t"], links["k"]
            steps = {}

            def stats(l, src, st_, mv_, signal):
                l.done(dve.bn_stats(st_[:], src[:]))
                l.wait_apart()
                l.done(dve.bn_aggr(mv_[:], st_[:]))
                l.wait()
                dve.tensor_scalar_add(mv_[:, 1:2], mv_[:, 1:2], 1e-5).then_inc(s[signal], 1)

            def normed(src, mv_, rs_, out, root, signal, free):
                def step(t):
                    dve.wait_ge(s[root], t + 1)
                    wait_past(dve, s[free], t)
                    dve.tensor_scalar(out[:], src[:], mv_[:, 0:1], rs_[:, 0:1], ALU.subtract, ALU.mult)\
                       .then_inc(s[signal], 1)
                return step

            def stats1(t):
                dve.wait_ge(s["x_in"], 16 * (t + 1))
                stats(lx, x, st, mv, "var1")
            steps["x.stats"] = stats1
            steps["x.norm"] = normed(x, mv, rstd, xn, "root1", "xn_ready", "xnT_ps")

            def low(name, filled, bank, dst, signal, high, carried):
                def step(t):
                    dve.wait_ge(s[filled], t + 1)
                    dve.wait_ge(s[high], t + 1)
                    if carried:
                        wait_past(dve, s[carried], t)
                    dve.tensor_tensor(dst[:, 1, :], bank[:, 0:128], dst[:, 0, :], ALU.subtract)\
                        .then_inc(s[signal], 1)
                steps[name] = step
            low("x.low", "xnT_ps", x0, xnT, "xnL_sb", "xnT_sb", None)
            low("k.low", "xn3T_ps", t1, xn3K, "xn3L_sb", "xn3T_sb", "usE_ready")

            def take_q(k):
                def step(t):
                    dve.wait_ge(s["q_ps"], 4 * t + k + 1)
                    dve.tensor_scalar_mul(q[:, :, 4 * k:4 * k + 4, :].rearrange("c b h q -> c h b q"),
                                          x0[0:CD, :].rearrange("c (h b q) -> c h b q", h=4, b=2), 1.0 / QSCALE)\
                        .then_inc(s["q0_taken"], 1)
                return step
            steps["x.q3"] = take_q(3)

            def maxes(k):
                def step(t):
                    dve.wait_ge(s["sc_ps"], 4 * t + k + 1)
                    dve.tensor_reduce(negmax[:, k, :], xbank[1 - k % 2].rearrange("p (i m) -> p i m", i=4),
                                      AX.X, ALU.max, negate=True).then_inc(s["max_done"], 1)
                return step

            def rrows(k):
                def step(t):
                    dve.wait_ge(s["exp_done"], 4 * t + k + 1)
                    dve.reciprocal(rrow[:, k, :], rowsum[:, k, :]).then_inc(s["rrow_done"], 1)
                return step
            for k in range(4):
                steps[f"x.x{k}"], steps[f"x.r{k}"] = maxes(k), rrows(k)

            def add_cross(t):
                dve.wait_ge(s["xo_ps"], t + 1)
                dve.wait_ge(s["xr_in"], 16 * (t + 1))
                wait_past(dve, s["x3_ready"], t)
                dve.tensor_tensor(x2[:], xr[:], x1[:, 0:D], ALU.add).then_inc(s["x2_ready"], 1)
                dve.wait_ge(s["x2_ready"], t + 1)
                stats(ly, x2, st2, mv2, "var2")
            steps["y.add"] = add_cross
            steps["y.norm2"] = normed(x2, mv2, rstd2, xn2, "root2", "xn2_ready", "xn2T_ps")

            def tree_norm(t):
                dve.wait_ge(s["actx_ps"], t + 1)
                m = t0[0:N, 0:AH * 18].rearrange("q (h b d) -> q h b d", h=AH, b=2)
                lt.done(dve.reciprocal(arz[:], m[:, :, :, AD]))
                lt.wait()
                for b in range(2):
                    ins = dve.tensor_tensor(actx[:, b, :].rearrange("q (h d) -> q h d", h=AH), m[:, :, b, 0:AD],
                                            arz[:, :, b].unsqueeze(2).to_broadcast([N, AH, AD]), ALU.mult)
                ins.then_inc(s["actx_ready"], 1)
            steps["t.norm"] = tree_norm

            def add_tree(t):
                dve.wait_ge(s["ao_ps"], t + 1)
                wait_past(dve, s["x3b_ready"], t)
                dve.tensor_tensor(x3[:], x2[:], t0[:, 0:D], ALU.add).then_inc(s["x3_ready"], 1)
                dve.wait_ge(s["x3_ready"], t + 1)
                stats(lt, x3, st3, mv3, "var3")
            steps["t.add"] = add_tree
            steps["t.norm3"] = normed(x3, mv3, rstd3, xn3, "root3", "xn3_ready", "xn3T_ps")

            t0k = t0.rearrange("p (k i) -> p k i", k=NQ)

            def split(t):
                dve.wait_ge(s["key_ps"], t + 1)
                dve.nop(nofuse=True)
                for k in range(NQ):
                    ins = dve.max(top[:, k, :], t0k[:, k, :])
                lk.done(ins)
                lk.wait()
                lk.done(dve.tensor_tensor(u[:], t0k, top[:, :, 0:1].to_broadcast([128, NQ, NSQ]), ALU.subtract))
                lk.done(dve.tensor_tensor(tops[:, :, 0:8], top[:], top[:, :, 0:1].to_broadcast([128, NQ, 8]),
                                          ALU.subtract))
                lk.wait()
                uh = u[:].rearrange("p (h e) i -> p h (e i)", h=FH)
                lk.done(dve.tensor_scalar_max(us[:, :, 0, :], uh, FLOOR))
                lk.wait()
                dve.scalar_tensor_tensor(out=us[:, :, 1, :], in0=uh, scalar=FLOOR, in1=us[:, :, 0, :],
                                         op0=ALU.max, op1=ALU.subtract).then_inc(s["us_ready"], 1)
            steps["k.split"] = split

            def tops2(t):
                lk.wait_apart()
                for k in range(NQ):
                    ins = dve.match_replace(u2[:, k, :], tops[:, k, 0:8], u[:, k, :], DROPPED)
                lk.done(ins)
                lk.wait_apart()
                for k in range(NQ):
                    ins = dve.max(tops[:, k, 8:16], u2[:, k, :])
                lk.done(ins)
            steps["k.tops"] = tops2

            def candidates(t):
                lk.wait()
                tv = tops[:].rearrange("p (h e) r -> p h e r", e=2)
                at, i = 0, 0
                while i <= TOPK:
                    w = CAND[i]
                    n = CAND.count(w)
                    shape = [128, FH, n, w]
                    dst = cand[:, :, at:at + n * w].rearrange("p h (n w) -> p h n w", n=n)
                    lk.done(dve.tensor_tensor(dst, tv[:, :, 0, i:i + n].unsqueeze(3).to_broadcast(shape),
                                              tv[:, :, 1, 0:w].unsqueeze(2).to_broadcast(shape), ALU.add))
                    at += n * w
                    i += n
                lk.wait_apart()
                for h in range(FH):
                    ins = dve.max(best[:, h, 0:8], cand[:, h, :])
                lk.done(ins)
                lk.wait_apart()
                for h in range(FH):
                    ins = dve.match_replace(cand2[:, h, :], best[:, h, 0:8], cand[:, h, :], DROPPED)
                lk.done(ins)
                lk.wait_apart()
                for h in range(FH):
                    ins = dve.max(best[:, h, 8:16], cand2[:, h, :])
                ins.then_inc(s["best_ready"], 1)
                dve.wait_ge(s["best_ready"], t + 1)
                wait_past(dve, s["usE_ready"], t)
                lk.done(dve.tensor_tensor(cut[:], best[:, :, TOPK - 1], best[:, :, TOPK], ALU.add))
                lk.wait()
                lk.done(dve.tensor_scalar_mul(cut[:], cut[:], 0.5))
            steps["k.cand"] = candidates

            def weight_sum(t):
                dve.wait_ge(s["ebest_done"], t + 1)
                lk.done(dve.reduce_sum(z[:], ebest[:], AX.X))
                lk.wait()
                dve.reciprocal(rz[:], z[:]).then_inc(s["rz_ready"], 1)
            steps["k.z"] = weight_sum

            def carry(t):
                dve.wait_ge(s["usT_sb"], t + 1)
                dve.wait_ge(s["lnz_ready"], t + 1)
                wait_past(dve, s["mw_done"], FH * t)
                wait_past(dve, s["h_ps"], t)
                dve.tensor_copy(xn3T[:], xn3K[:])
                dve.tensor_copy(lnzE[:], lnz[:])
                dve.tensor_copy(cutE[:], cut[:])
                dve.tensor_copy(usT[:], usK[:]).then_inc(s["usE_ready"], 1)
            steps["e.us"] = carry

            def mask(h):
                def step(t):
                    dve.wait_ge(s["ew_done"], FH * t + h + 1)
                    if h < NMW:
                        wait_past(dve, s["wsum_step"], (FH - 1) * t + h - (FH - 1 - NMW))
                    else:
                        dve.wait_ge(s["wsum_step"], (FH - 1) * t + max(h - NMW, 1))
                    dve.scalar_tensor_tensor(out=mw[:, h % NMW, :], in0=sslot[h][:, :], scalar=cutE[:, h:h + 1],
                                             in1=ew[:, h % 2, :], op0=ALU.is_ge, op1=ALU.mult)\
                       .then_inc(s["mw_done"], 1)
                return step
            for h in range(FH):
                steps[f"e.w{h}"] = mask(h)

            def add_experts(t):
                dve.wait_ge(s["y_ps"], t + 1)
                wait_past(dve, s["out_done"], 16 * t)
                dve.tensor_tensor(y[:], x3c[:], f0[:, 0:D], ALU.add).then_inc(s["y_ready"], 1)
            steps["e.add"] = add_experts

            def begin(stage, t):
                if stage in links:
                    links[stage].begin(t)
            run(dve, steps, DVE_ORDER, begin)
            assert all(l.n == l.per_tile for l in links.values()), [l.n for l in links.values()]

        @block.gpsimd
        def _(pool):
            pool.memset(halfneg[:], -0.5).then_inc(s["pool_set"], 1)
            pool.memset(feat[:, :, 0:1], 1.0).then_inc(s["pool_set"], 1)
            pool.memset(vblk[:], 0.0).then_inc(s["pool_set"], 1)
            pool.wait_ge(s["pool_set"], 3)
            for b in range(2):
                pool.memset(vblk[N * b:N * b + N, :, b, AD:AD + 1], 1.0).then_inc(s["pool_set"], 1)
            pool.wait_ge(s["pool_set"], 5)
            pool.wait_ge(s["wload"], 16 * (len(WEIGHTS) - 2))
            steps = {}

            def root(variance, mv_, rs_, signal):
                def step(t):
                    pool.wait_ge(s[variance], t + 1)
                    pool.tensor_tensor(rs_[:], mv_[:, 1:2], halfneg[:], ALU.pow).then_inc(s[signal], 1)
                return step
            steps["x.root"] = root("var1", mv, rstd, "root1")
            steps["y.root2"] = root("var2", mv2, rstd2, "root2")
            steps["t.root3"] = root("var3", mv3, rstd3, "root3")

            def norm(k):
                def step(t):
                    pool.wait_ge(s["rrow_done"], 4 * t + k + 1)
                    pool.tensor_tensor(p[:, k, :, :], p[:, k, :, :],
                                       rrow[:, k, :].unsqueeze(2).to_broadcast([128, 4, M]), ALU.mult)\
                        .then_inc(s["norm_done"], 1)
                return step
            for k in range(4):
                steps[f"x.n{k}"] = norm(k)

            def features(t):
                pool.wait_ge(s["alpha_done"], t + 1)
                for l in range(DEPTH):
                    w = 2 ** l
                    ins = pool.tensor_tensor(feat[:, :, w:2 * w], feat[:, :, 0:w],
                                             alpha[:, :, l:l + 1].to_broadcast([128, AH, w]), ALU.mult)
                    if l < DEPTH - 1:
                        ins.then_inc(s["pool_t"], 1)
                        pool.wait_ge(s["pool_t"], (DEPTH - 1) * t + l + 1)
                ins.then_inc(s["feat_ready"], 1)
            steps["t.feat"] = features

            def keep(src, dst, filled, reader, signal):
                def step(t):
                    pool.wait_ge(s[filled], t + 1)
                    wait_past(pool, s[reader], t)
                    pool.nop(nofuse=True)
                    pool.tensor_copy(dst[:], src[:]).then_inc(s[signal], 1)
                return step
            steps["k.keep"] = keep(x3, x3b, "x3_ready", "x3c_ready", "x3b_ready")
            steps["e.keep"] = keep(x3b, x3c, "x3b_ready", "y_ready", "x3c_ready")

            def add_weights(h):
                def step(t):
                    pool.wait_ge(s["mw_done"], FH * t + h + 1)
                    if h == 1:
                        wait_past(pool, s["g_ready"], t)
                    else:
                        pool.wait_ge(s["wsum_step"], (FH - 1) * t + h - 1)
                    pool.tensor_tensor(wsum[:], mw[:, 0, :] if h == 1 else wsum[:], mw[:, h % NMW, :],
                                       ALU.add).then_inc(s["wsum_step"], 1)
                return step
            for h in range(1, FH):
                steps[f"e.a{h}"] = add_weights(h)

            def gate(t):
                pool.wait_ge(s["wsum_step"], (FH - 1) * (t + 1))
                pool.wait_ge(s["gelu_done"], t + 1)
                wait_past(pool, s["gT_ps"], t)
                pool.tensor_tensor(g[:], wsum[:], gh[:], ALU.mult).then_inc(s["g_ready"], 1)
            steps["e.gate"] = gate
            run(pool, steps, POOL_ORDER)


PE_ORDER = """
    y.m0 y.m1 y.m2 y.m3 e.s0 e.s1 y.out x.turn k.turn3 e.s2 e.s3 x.q0 t.turn x.q1 t.pv e.hid k.key x.q2 e.s4
    x.q3 e.s5 k.kturn e.s6 t.feat x.s0 e.s7 x.s1 t.sim x.s2 x.s3 t.mix e.gturn x.p0 t.cturn x.p1 e.out x.p2
    x.p3 t.out
""".split()
ACT_ORDER = """
    y.m0 y.m1 y.m2 y.m3 e.e0 e.e1 x.turn k.turn3 e.e2 t.turn x.q0 x.q1 e.e3 t.v t.alpha e.gelu e.e4 e.e5
    k.kturn x.q2 e.e6 t.feat e.e7 x.e0 x.e1 t.exp x.e2 x.e3 e.gturn t.cturn x.p0 x.p1 x.p2 k.ebest x.p3
    k.lnz
""".split()
DVE_ORDER = """
    e.us x.stats x.norm e.w0 e.w1 y.add x.low k.low y.norm2 e.w2 e.w3 k.split e.w4 x.q3 e.w5 e.w6 x.x0 x.x1
    e.w7 k.tops x.x2 x.r0 x.x3 x.r1 x.r2 t.norm x.r3 k.cand k.z t.add e.add t.norm3
""".split()
POOL_ORDER = """
    e.keep k.keep x.root y.root2 e.a1 e.a2 e.a3 t.feat e.a4 e.a5 e.a6 e.a7 e.gate x.n0 x.n1 x.n2 x.n3
    t.root3
""".split()



def kernel(**inputs):
    import concourse.bacc as bacc
    from concourse.bass_utils import run_bass_kernel_spmd

    w = {k: np.asarray(v) for k, v in inputs.items()}
    cc = np.ascontiguousarray
    keys = np.zeros((128, 4, 2 * NSQ), np.float32)
    for i in range(4):
        keys[32 * i:32 * i + DQH, i, 0:NSQ] = w["L0_ffn_K1"].T
        keys[32 * i + DQH:32 * i + 2 * DQH, i, NSQ:] = w["L0_ffn_K2"].T
    pair = np.arange(NE)
    one = np.concatenate([np.arange(NSQ)[:, None] == pair // NSQ, np.arange(NSQ)[:, None] == pair % NSQ])
    last = np.array([0] + [f.bit_length() for f in range(1, NF)])
    weight = np.array([sum(2.0 ** -d for d in range(max(l, 1), DEPTH + 1)) for l in last]) / DEPTH
    arrays = {
        "x": cc(w["x"].reshape(B * N, D)), "c": cc(w["ctx_768"]), "cT": cc(w["ctx_768"].transpose(0, 2, 1)),
        "ident": np.eye(128, dtype=np.float32), "ident16": np.eye(128, dtype=np.float16),
        "sel": np.concatenate([one, one]).astype(np.float16),
        "cneg": np.tile(np.where(np.arange(N)[None, :] >= (np.arange(128) % N)[:, None], 0.0, FLOOR), (1, AHP)).astype(np.float16),
        "rootc": np.tile(np.sqrt(weight), 2).astype(np.float32)[:, None],
        "wqT": cc(w["L0_xattn_Wq"].T), "wkT": cc(w["L0_xattn_Wk"].T), "wvT": cc(w["L0_xattn_Wv"].T),
        "wo": cc(w["L0_xattn_Wo"]), "bo": np.tile(w["L0_xattn_bo"], (96, 1)),
        "wp": w["L0_attn_Wp"], "bp": np.tile(w["L0_attn_bp"], (96, 1)), "awv": w["L0_attn_Wv"], "awo": w["L0_attn_Wo"],
        "fwqT": cc(w["L0_ffn_Wq"].T), "fbqT": np.repeat(w["L0_ffn_bq"].reshape(2, 128).T[:, :, None], 96, 2), "keys": keys,
        "wdT": cc(w["L0_ffn_W_down"][0:NE].T), "wup": cc(w["L0_ffn_W_up"][0:NE]),
    }
    nc = bacc.Bacc("TRN2", target_bir_lowering=False, num_devices=1)
    aps = {k: nc.dram_tensor(k + "_dram", v.shape, mybir.dt.from_np(v.dtype), kind="ExternalInput").ap()
           for k, v in arrays.items()}
    aps["y"] = nc.dram_tensor("y_dram", (B * N, D), mybir.dt.float32, kind="ExternalOutput").ap()
    build(nc, aps)
    r = run_bass_kernel_spmd(nc, [{k + "_dram": v for k, v in arrays.items()}], core_ids=[0])
    return r.results[0]["y_dram"].reshape(B, N, D)
```
